# Optimizing a Trainium2 kernel written in Bass

```python
import numpy as np
import jax
import jax.numpy as jnp

def _softmax(x, axis=-1):
    return jax.nn.softmax(x, axis=axis)

def _gelu(x):
    return jax.nn.gelu(x, approximate=True)

def _silu(x):
    return jax.nn.silu(x)

def _sigmoid(x):
    return jax.nn.sigmoid(x)

def _layernorm(x, axis=-1, eps=1e-05):
    m = jnp.mean(x, axis=axis, keepdims=True)
    v = jnp.var(x, axis=axis, keepdims=True)
    return (x - m) / jnp.sqrt(v + eps)

def _scatter_add(tgt, idx, src, axis=0):
    return tgt.at[idx].add(src)

def _segment_sum(src, seg, n):
    return jax.ops.segment_sum(src, seg, n)
kernel_name = 'mk_flamingo_gated_d1_seqx_r4_c8a348'

def setup_inputs(seed: int=0):
    np.random.seed(seed)
    _w = jnp.asarray

    def _rec_inputs():
        import jax
        import jax.numpy as jnp
        _rk = jax.random.key(seed)
        x = -0.0002928 + 1 * jax.random.normal(jax.random.fold_in(_rk, 1), (4, 512, 256), jnp.float32)
        _lenS = 512 - jax.random.randint(jax.random.fold_in(_rk, 7), (4,), 0, max(1, 512 // 4) + 1, jnp.int32)
        _lenS2 = 512 - jax.random.randint(jax.random.fold_in(_rk, 8), (4,), 0, max(1, 512 // 4) + 1, jnp.int32)
        _ctx_1024P = jax.random.normal(jax.random.fold_in(_rk, 11), (4, 16, 256), jnp.float32)
        _ctx_1024c = jax.random.dirichlet(jax.random.fold_in(_rk, 511), 0.3 * jnp.ones((16,), jnp.float32), (4, 512))
        _ctx_1024t = jnp.einsum('bsk,bkd->bsd', _ctx_1024c, _ctx_1024P)
        _ctx_1024t = _ctx_1024t * jax.lax.rsqrt(jnp.mean(jnp.square(_ctx_1024t)) + 1e-12) * 0.953939
        ctx_1024 = -1.39393e-06 + 0.999914 * (_ctx_1024t + 0.3 * jax.random.normal(jax.random.fold_in(_rk, 611), (4, 512, 256), jnp.float32))
        _g = jax.random.normal(jax.random.fold_in(_rk, 9001), (2, 1), jnp.float32)
        _g = jnp.sign(_g) * jnp.maximum(jnp.abs(_g), 1.0) + (_g == 0) * 1.0
        g_xattn = _g[0]
        g_ffn = _g[1]
        return (x, ctx_1024, g_xattn, g_ffn)
    x, ctx_1024, g_xattn, g_ffn = _rec_inputs()

    def _L0_xattn_setup():
        import jax, jax.numpy as jnp
        import numpy as np
        B, L, DIM = (2, 512, 256)
        H, DH, W = (16, 64, 64)
        ROPE_BASE = 10000.0

        def _rope(x):
            l, d = (x.shape[1], x.shape[3])
            freqs = 1.0 / ROPE_BASE ** (jnp.arange(0, d, 2, dtype=jnp.float32) / d)
            ang = jnp.arange(l, dtype=jnp.float32)[:, None] * freqs[None, :]
            cos = jnp.cos(ang)[None, :, None, :].astype(x.dtype)
            sin = jnp.sin(ang)[None, :, None, :].astype(x.dtype)
            xe, xo = (x[..., 0::2], x[..., 1::2])
            ye = xe * cos - xo * sin
            yo = xe * sin + xo * cos
            return jnp.stack([ye, yo], axis=-1).reshape(x.shape)
        key = jax.random.key(seed)
        ks = jax.random.split(key, 7)
        sh = (B, L, DIM)
        return {'q': jax.random.normal(ks[0], sh, jnp.float32), 'k': jax.random.normal(ks[1], sh, jnp.float32), 'v': jax.random.normal(ks[2], sh, jnp.float32), 'wq': jax.random.normal(ks[3], (H * DH, DIM), jnp.float32) * 0.02, 'wk': jax.random.normal(ks[4], (H * DH, DIM), jnp.float32) * 0.02, 'wv': jax.random.normal(ks[5], (H * DH, DIM), jnp.float32) * 0.02, 'wo': jax.random.normal(ks[6], (DIM, H * DH), jnp.float32) * 0.02}
    _L0_xattn_all = _L0_xattn_setup()
    _L0_xattn_in = {k: v for k, v in _L0_xattn_all.items() if k in ('wq', 'wk', 'wv', 'wo')}
    del _L0_xattn_all

    def _L0_ffn_setup():
        import jax, jax.numpy as jnp
        import numpy as np
        H_DIM, E_DIM = (256, 128)
        N_SHARED, N_ROUTED, TOP_K = (2, 16, 4)
        B, S = (4, 512)
        key = jax.random.key(seed)
        ks = jax.random.split(key, 6)
        sc = 1.0 / np.sqrt(H_DIM)
        ec = 1.0 / np.sqrt(E_DIM)
        return {'x': jax.random.normal(ks[0], (B, S, H_DIM), dtype=jnp.float32), 'shared_up': jax.random.uniform(ks[1], (N_SHARED, E_DIM, H_DIM), jnp.float32, -sc, sc), 'shared_down': jax.random.uniform(ks[2], (N_SHARED, H_DIM, E_DIM), jnp.float32, -ec, ec), 'routed_up': jax.random.uniform(ks[3], (N_ROUTED, E_DIM, H_DIM), jnp.float32, -sc, sc), 'routed_down': jax.random.uniform(ks[4], (N_ROUTED, H_DIM, E_DIM), jnp.float32, -ec, ec), 'router_w': jax.random.uniform(ks[5], (N_ROUTED, H_DIM), jnp.float32, -sc, sc)}
    _L0_ffn_all = _L0_ffn_setup()
    _L0_ffn_in = {k: v for k, v in _L0_ffn_all.items() if k in ('shared_up', 'shared_down', 'routed_up', 'routed_down', 'router_w')}
    del _L0_ffn_all
    return {'x': x, 'ctx_1024': ctx_1024, 'g_xattn': g_xattn, 'g_ffn': g_ffn, 'L0_xattn_wq': _L0_xattn_in['wq'], 'L0_xattn_wk': _L0_xattn_in['wk'], 'L0_xattn_wv': _L0_xattn_in['wv'], 'L0_xattn_wo': _L0_xattn_in['wo'], 'L0_ffn_shared_up': _L0_ffn_in['shared_up'], 'L0_ffn_shared_down': _L0_ffn_in['shared_down'], 'L0_ffn_routed_up': _L0_ffn_in['routed_up'], 'L0_ffn_routed_down': _L0_ffn_in['routed_down'], 'L0_ffn_router_w': _L0_ffn_in['router_w']}

def reference(x, ctx_1024, g_xattn, g_ffn, L0_xattn_wq, L0_xattn_wk, L0_xattn_wv, L0_xattn_wo, L0_ffn_shared_up, L0_ffn_shared_down, L0_ffn_routed_up, L0_ffn_routed_down, L0_ffn_router_w):
    import jax
    import jax.numpy as jnp

    def _L0_xattn_ref(q, k, v, wq, wk, wv, wo):
        import jax, jax.numpy as jnp
        import numpy as np
        B, L, DIM = (2, 512, 256)
        H, DH, W = (16, 64, 64)
        ROPE_BASE = 10000.0

        def _rope(x):
            l, d = (x.shape[1], x.shape[3])
            freqs = 1.0 / ROPE_BASE ** (jnp.arange(0, d, 2, dtype=jnp.float32) / d)
            ang = jnp.arange(l, dtype=jnp.float32)[:, None] * freqs[None, :]
            cos = jnp.cos(ang)[None, :, None, :].astype(x.dtype)
            sin = jnp.sin(ang)[None, :, None, :].astype(x.dtype)
            xe, xo = (x[..., 0::2], x[..., 1::2])
            ye = xe * cos - xo * sin
            yo = xe * sin + xo * cos
            return jnp.stack([ye, yo], axis=-1).reshape(x.shape)
        b, l, _ = q.shape
        qh = (q @ wq.T).reshape(b, l, H, DH)
        kh = (k @ wk.T).reshape(b, l, H, DH)
        vh = (v @ wv.T).reshape(b, l, H, DH).transpose(0, 2, 1, 3)
        qh = _rope(qh).transpose(0, 2, 1, 3)
        kh = _rope(kh).transpose(0, 2, 1, 3)
        scores = jnp.einsum('bhqd,bhkd->bhqk', qh, kh) * DH ** (-0.5)
        i = jnp.arange(l)[:, None]
        j = jnp.arange(l)[None, :]
        window_mask = (j <= i) & (j >= i - W)
        scores = jnp.where(window_mask, scores, -1e+30)
        probs = jax.nn.softmax(scores, axis=-1)
        out = jnp.einsum('bhqk,bhkd->bhqd', probs, vh)
        out = out.transpose(0, 2, 1, 3).reshape(b, l, H * DH)
        return out @ wo.T

    def _L0_ffn_ref(x, shared_up, shared_down, routed_up, routed_down, router_w):
        import jax, jax.numpy as jnp
        import numpy as np
        H_DIM, E_DIM = (256, 128)
        N_SHARED, N_ROUTED, TOP_K = (2, 16, 4)
        B, S = (4, 512)
        b, s, h = x.shape
        xt = x.reshape(-1, h)
        up_s = jnp.einsum('th,seh->tse', xt, shared_up)
        shared = jnp.einsum('tse,she->th', jax.nn.gelu(up_s, approximate=False), shared_down)
        probs = jax.nn.softmax(xt @ router_w.T, axis=-1)
        topk_p, topk_i = jax.lax.top_k(probs, TOP_K)
        gate = jnp.zeros_like(probs).at[jnp.arange(xt.shape[0])[:, None], topk_i].add(topk_p)
        up_r = jnp.einsum('th,reh->tre', xt, routed_up)
        act = jax.nn.gelu(up_r, approximate=False) * gate[:, :, None]
        routed = jnp.einsum('tre,rhe->th', act, routed_down)
        return (shared + routed).reshape(b, s, h)
    x = x + jnp.tanh(g_xattn[0]) * _L0_xattn_ref(_layernorm(x, axis=-1), ctx_1024, ctx_1024, L0_xattn_wq, L0_xattn_wk, L0_xattn_wv, L0_xattn_wo)
    x = x + jnp.tanh(g_ffn[0]) * _L0_ffn_ref(_layernorm(x, axis=-1), L0_ffn_shared_up, L0_ffn_shared_down, L0_ffn_routed_up, L0_ffn_routed_down, L0_ffn_router_w)
    return x

_drawn_inputs = setup_inputs


def setup_inputs(seed=0):
    import zlib

    import numpy as np

    out = dict(_drawn_inputs(seed))
    spreads = {}
    factors = {'L0_xattn_wq': 8.0, 'L0_xattn_wk': 8.0}
    for name, (base, spread) in spreads.items():
        noise = np.random.default_rng([zlib.crc32(name.encode()), seed]).standard_normal(out[name].shape)
        drawn = base * np.exp(spread * noise) if base else spread * noise
        out[name] = jnp.asarray(drawn.astype(out[name].dtype))
    for name, factor in factors.items():
        out[name] = (out[name] * factor).astype(out[name].dtype)
    return out
```

```python
from contextlib import ExitStack

import numpy as np

from concourse import mybir

F32 = mybir.dt.float32
F32R = mybir.dt.float32r
ALU = mybir.AluOpType
ACT = mybir.ActivationFunctionType
AX_X = mybir.AxisListType.X

P = 128
B, L, D = 4, 512, 256
H, DH, W = 16, 64, 64
HALF = DH // 2
ROPE_BASE = 10000.0
KC = D // P
TT = L // P
G = 4
GD = G * DH
GROUPS = H // G
UNITS = B * GROUPS
CHUNKS = UNITS * G
NS, NR, TOPK = 2, 16, 4
NE = NS + NR
SENT = 8 - TOPK
EPS = 1e-5
SCALE = float(DH) ** -0.5
MASKED = -1e30
PIECE = KC * D
WPIECES = 4 * GROUPS
RAW = 4


def products(stationary, moving):
    (sh, sl), (mh, ml) = stationary, moving
    return ((sh, mh), (sh, ml), (sl, mh))


def build(nc, x_d, ctx_d, gx_d, gf_d, w_d, e_d, rw_d, cos_d, sin_d, mask_d, ident_d, out_d):
    with ExitStack() as ctx:
        def sb(name, shape, dt=F32):
            return ctx.enter_context(nc.sbuf_tensor(name, shape, dt))

        def sem(name):
            return ctx.enter_context(nc.semaphore(name))

        x = sb("x", [P, B, TT, D])
        wh = sb("wh", [P, NE, PIECE], F32R)
        wl = sb("wl", [P, NE, PIECE], F32R)
        raw = sb("raw", [P, RAW, PIECE])
        xTh = [sb(f"xTh{i}", [P, KC, L], F32R) for i in range(2)]
        xTl = [sb(f"xTl{i}", [P, KC, L], F32R) for i in range(2)]
        craw = sb("craw", [P, KC, L])
        cos = sb("cos", [P, L])
        sin = sb("sin", [P, 2, L])
        mask = sb("mask", [P, 2, P])
        ident = sb("ident", [P, P])
        xn = sb("xn", [P, TT, D])
        stats = sb("stats", [P, TT, 6])
        mv = sb("mv", [P, TT, 2])
        vare = sb("vare", [P, TT])
        rstd = sb("rstd", [P, TT])
        mhalf = sb("mhalf", [P, TT])
        gates_in = sb("gates_in", [P, 2])
        tg = sb("tg", [P, 2])
        rw = sb("rw", [P, KC, NR])
        rwh = sb("rwh", [P, KC, NR], F32R)
        rwl = sb("rwl", [P, KC, NR], F32R)
        sizes = dict(rot1=(2, 2, L), rot2=(2, 2, L), qT=(2, 2, L), kT=(2, 2, W + L),
                     v_al=(2, TT, GD), v_sh=(2, TT, GD))
        arena = sb("arena", [P, sum(int(np.prod(s)) for s in sizes.values())])
        cuts, at = {}, 0
        for name, (a, b, c) in sizes.items():
            cuts[name] = arena[:, at:at + a * b * c].rearrange("p (a b c) -> p a b c", a=a, b=b)
            at += a * b * c
        rot1, rot2 = cuts["rot1"], cuts["rot2"]
        qT, kT = cuts["qT"], cuts["kT"]
        v_al, v_sh = cuts["v_al"], cuts["v_sh"]
        gate_bc = arena[:, 0:NR * L].rearrange("p (e n) -> p e n", e=NR)
        sneg = sb("sneg", [P, 2, TT, P])
        prob = sb("prob", [P, 2, TT, P])
        pT = sb("pT", [P, 2, TT, P])
        nmax = sb("nmax", [P, 4, TT])
        rsum = sb("rsum", [P, 4, TT])
        rinv = sb("rinv", [P, 2, TT])
        att = sb("att", [P, 2, TT, GD])
        oTh = sb("oTh", [P, 2, L], F32R)
        oTl = sb("oTl", [P, 2, L], F32R)
        act_g = sneg[:, :, :, :].rearrange("p a t c -> p a (t c)")
        act_f = prob[:, :, :, :].rearrange("p a t c -> p a (t c)")
        lmax = sb("lmax", [P, TT])
        lex = sb("lex", [P, TT, NR])
        lexp = sb("lexp", [P, TT, NR])
        lsum = sb("lsum", [P, TT])
        linv = sb("linv", [P, TT])
        pr = sb("pr", [P, TT, NR + SENT])
        top = sb("top", [P, TT, 8])
        rep = sb("rep", [P, TT, NR + SENT])
        gate = sb("gate", [P, TT, NR])
        gT = craw[0:NR, 0, :]
        gT_d = nc.dram_tensor("gate_scratch", (B, NR, L), F32).ap()

        ring = [ctx.enter_context(nc.psum_tensor(f"ring{i}", [P, 2, L], F32)) for i in range(2)]
        psS = [ctx.enter_context(nc.psum_tensor(f"psS{i}", [P, TT, P], F32)) for i in range(2)]
        psT = ctx.enter_context(nc.psum_tensor("psT", [P, TT, P], F32))
        psO = ctx.enter_context(nc.psum_tensor("psO", [P, 2, TT, DH], F32))

        in_x = [sem(f"in_x{b}") for b in range(B)]
        in_ctx = sem("in_ctx")
        in_raw = [sem(f"in_raw{i}") for i in range(RAW)]
        in_const = sem("in_const")
        pool_init = sem("pool_init")
        w_hi = sem("w_hi")
        w_lo_v = sem("w_lo_v")
        w_lo_p = sem("w_lo_p")
        rw_hi, rw_lo = sem("rw_hi"), sem("rw_lo")
        c_hi, c_lo = sem("c_hi"), sem("c_lo")
        tg_done = sem("tg_done")
        ln_stat = sem("ln_stat")
        ln_rstd = sem("ln_rstd")
        ln_norm = sem("ln_norm")
        xT_pe, xT_hi, xT_lo = sem("xT_pe"), sem("xT_hi"), sem("xT_lo")
        qk_pe, qk_mul, qk_add = sem("qk_pe"), sem("qk_mul"), sem("qk_add")
        q_in = [sem(f"q_in{i}") for i in range(2)]
        k_in = [sem(f"k_in{i}") for i in range(2)]
        v_pe, v_out = sem("v_pe"), sem("v_out")
        v_in = [sem(f"v_in{i}") for i in range(2)]
        s_pe, s_max, s_exp = sem("s_pe"), sem("s_max"), sem("s_exp")
        p_pe, p_out = sem("p_pe"), sem("p_out")
        o_pe, o_inv, o_out = sem("o_pe"), sem("o_inv"), sem("o_out")
        oT_pe, oT_hi, oT_lo = sem("oT_pe"), sem("oT_hi"), sem("oT_lo")
        y_pe, y_out = sem("y_pe"), sem("y_out")
        dve_link, pool_link = sem("dve_link"), sem("pool_link")
        r_pe, r_sub, r_exp, r_gate = sem("r_pe"), sem("r_sub"), sem("r_exp"), sem("r_gate")
        gT_pe, gT_out, gT_dram = sem("gT_pe"), sem("gT_out"), sem("gT_dram")
        gate_in = [sem(f"gate_in{i}") for i in range(NR)]
        up_pe, f_gelu, f_mul = sem("up_pe"), sem("f_gelu"), sem("f_mul")
        f_hi, f_lo, down_pe = sem("f_hi"), sem("f_lo"), sem("down_pe")
        z_out, out_done = sem("z_out"), sem("out_done")

        def slot(i):
            return i if i < NE else i - NE

        def expert_piece(e):
            return WPIECES + e

        prologue = ([("stat", 0), ("w", 0), ("norm", 0), ("xT", 0), ("w", 1), ("q", 0), ("ctx", 0), ("w", 2),
                     ("k", 0), ("v", 0)] + [("w", i) for i in range(3, 8)])
        steps = []
        for c in range(CHUNKS + 4):
            u, k = divmod(c, 4)
            b, g = divmod(u, GROUPS)
            jobs = []
            if k == 0 and u + 1 < UNITS:
                jobs.append(("q", u + 1))
            if k == 1 and u + 1 < UNITS:
                jobs += [("k", u + 1), ("v", u + 1)]
            if k == 2 and u >= 1:
                jobs.append(("oT", u - 1))
            if k == 2 and g == 2 and b + 1 < B:
                jobs += [("xT", b + 1), ("ctx", b + 1)]
            if k == 3 and u >= 1:
                jobs.append(("y", u - 1))
            if u < 2 and k >= 2:
                jobs += [("w", 8 + 4 * u + 2 * (k - 2)), ("w", 9 + 4 * u + 2 * (k - 2))]
            if k == 3 and g == 1 and b + 1 < B:
                jobs.append(("stat", b + 1))
            if k == 0 and g == 2 and b + 1 < B:
                jobs.append(("norm", b + 1))
            jobs += {(UNITS - 2, 2): [("stat", B)], (UNITS - 2, 3): [("norm", B)],
                     (UNITS - 1, 0): [("xT", B)], (UNITS - 1, 1): [("r", 0)],
                     (UNITS - 1, 3): [("gT", 0)]}.get((u, k), [])
            if (u, k) == (UNITS - 4, 0):
                jobs += [("w", expert_piece(e)) for e in range(NS)]
            if k == 0 and u >= UNITS - 2:
                first = NS + 4 * (u - (UNITS - 2))
                jobs += [("w", expert_piece(e)) for e in range(first, first + 4)]
            steps.append((c, jobs))
        experts = [(b, e) for b in range(B) for e in range(NE)]
        N = len(experts)
        after = {n: [] for n in range(N + 2)}
        after[0] += [("w", expert_piece(e)) for e in range(NE - 4, NE)]
        for b in range(B - 1):
            for e, kind in ((1, "stat"), (2, "norm"), (4, "xT"), (7, "r"), (10, "gT")):
                after[b * NE + e].append((kind, b + 1 + (B if kind in ("stat", "norm", "xT") else 0)))
        for b in range(B):
            after[b * NE + NE + 1].append(("z", b))

        in_ring = ("xT", "q", "k", "v", "oT", "y", "r", "gT")
        jobs_a = [j for jobs in [prologue] + [jobs for _, jobs in steps] for j in jobs]
        ring_jobs = [j for j in jobs_a if j[0] in in_ring]
        ring_at = {j: n for n, j in enumerate(ring_jobs)}

        def banks(job):
            if job in ring_at:
                r = ring[ring_at[job] % 2]
                return [r[:, 0, :], r[:, 1, :]]
            return [psT[:, :, :].rearrange("p t c -> p (t c)"),
                    psO[:, :, :, :].rearrange("p a t d -> p (a t d)")]

        def both_banks(job):
            return ring[ring_at[job] % 2]

        def released(job):
            kind, n = job
            return {"xT": (xT_lo, n + 1), "q": (qk_mul, 2 * n + 1), "k": (qk_mul, 2 * n + 2),
                    "v": (v_out, n + 1), "oT": (oT_lo, n + 1), "y": (y_out, n + 1),
                    "r": (r_sub, n + 1), "gT": (gT_out, n + 1)}[kind]

        def fillings(u):
            return u // 2 + 1

        def side(j):
            return 0 if j < B else (j - B) % 2

        def wait_w_lo(eng, i):
            if i < 3:
                eng.wait_ge(w_lo_v, i + 1)
            else:
                eng.wait_ge(w_lo_p, i - 2)

        def wait_slot_free(eng, i):
            if i >= NE:
                g, m = divmod(slot(i), 4)
                eng.wait_ge(y_pe if m == 3 else v_pe, (B - 1) * GROUPS + g + 1)

        consts = 16 * 7
        block = ctx.enter_context(nc.Block())

        @block.sync
        def _(sp):
            def load_piece(i):
                if i >= RAW:
                    sp.wait_ge(w_hi, i - RAW + 1)
                    wait_w_lo(sp, i - RAW)
                src = w_d[i] if i < WPIECES else e_d[i - WPIECES]
                sp.dma_start(raw[:, i % RAW, :], src).then_inc(in_raw[i % RAW], 16)

            def load_ctx(b):
                if b:
                    sp.wait_ge(c_lo, b)
                sp.dma_start(craw[:, :, :], ctx_d[b]).then_inc(in_ctx, 16)

            def lay_heads(u, is_k):
                i = 2 * u + is_k
                sp.wait_ge(qk_add, i + 1)
                if u >= 2:
                    sp.wait_ge(s_pe, G * (u - 1))
                if is_k and u < 2:
                    sp.wait_ge(pool_init, 1)
                for h in range(G):
                    for half in range(2):
                        row = (h % 2) * DH + half * HALF
                        dst = (kT[row:row + HALF, u % 2, h // 2, W:W + L] if is_k
                               else qT[row:row + HALF, u % 2, h // 2, :])
                        sp.dma_start(dst, rot1[h * HALF:(h + 1) * HALF, i % 2, half, :]
                                     ).then_inc((k_in if is_k else q_in)[u % 2], 16)

            def shift_values(u):
                sp.wait_ge(v_out, u + 1)
                sp.dma_start(v_sh[W:P, u % 2, :, :], v_al[0:W, u % 2, :, :]).then_inc(v_in[u % 2], 16)
                sp.dma_start(v_sh[0:W, u % 2, 1:TT, :],
                             v_al[W:P, u % 2, 0:TT - 1, :]).then_inc(v_in[u % 2], 16)

            def spread_gates(b):
                sp.wait_ge(gT_out, b + 1)
                sp.dma_start(gT_d[b], gT).then_inc(gT_dram, 16)
                sp.wait_ge(gT_dram, 16 * (b + 1))
                for r in range(NR):
                    if b:
                        sp.wait_ge(f_mul, (b - 1) * NR + r + 1)
                    elif r == 0:
                        sp.wait_ge(s_pe, CHUNKS)
                    sp.dma_start(gate_bc[:, r, :],
                                 gT_d[b, r].partition_broadcast(P)).then_inc(gate_in[r], 16)

            sp.dma_start(x[:, 0, :, :], x_d[0]).then_inc(in_x[0], 16)
            sp.dma_start(ident[:, :], ident_d).then_inc(in_const, 16)
            for i in range(3):
                load_piece(i)
            load_ctx(0)
            load_piece(3)
            for dst, src in ((cos[:, :], cos_d), (sin[:, :, :], sin_d), (mask[:, :, :], mask_d),
                             (rw[:, :, :], rw_d), (gates_in[:, 0:1], gx_d.partition_broadcast(P)),
                             (gates_in[:, 1:2], gf_d.partition_broadcast(P))):
                sp.dma_start(dst, src).then_inc(in_const, 16)
            for b in range(1, B):
                sp.dma_start(x[:, b, :, :], x_d[b]).then_inc(in_x[b], 16)

            def store(b):
                sp.wait_ge(z_out, b + 1)
                sp.dma_start(out_d[b], x[:, b, :, :]).then_inc(out_done, 16)

            def do(job):
                kind, n = job
                if kind == "w" and n + RAW < WPIECES + NE:
                    load_piece(n + RAW)
                elif kind == "ctx" and n + 1 < B:
                    load_ctx(n + 1)
                elif kind in "qk":
                    lay_heads(n, kind == "k")
                elif kind == "v":
                    shift_values(n)
                elif kind == "gT":
                    spread_gates(n)
                elif kind == "z":
                    store(n)

            for job in jobs_a + [j for n in range(N + 2) for j in after[n]]:
                do(job)
            sp.wait_ge(out_done, 16 * B)

        @block.gpsimd
        def _(pool):
            links = [0]

            def link(ins):
                links[0] += 1
                ins.then_inc(pool_link, 1)
                pool.wait_ge(pool_link, links[0])

            pool.memset(kT[:, :, :, 0:W], 0.0)
            pool.memset(v_sh[0:W, :, 0, :], 0.0)
            pool.memset(pr[:, :, NR:], -1.0)
            pool.memset(mhalf[:, :], -0.5).then_inc(pool_init, 1)
            pool.wait_ge(pool_init, 1)

            def do(job):
                kind, n = job
                if kind == "w" and n >= 3:
                    pool.wait_ge(w_hi, n + 1)
                    pool.tensor_tensor(wl[:, slot(n), :], raw[:, n % RAW, :],
                                       wh[:, slot(n), :].bitcast(F32),
                                       ALU.subtract).then_inc(w_lo_p, 1)
                elif kind == "ctx":
                    pool.wait_ge(c_hi, n + 1)
                    pool.tensor_tensor(xTl[1][:, :, :], craw[:, :, :], xTh[1][:, :, :].bitcast(F32),
                                       ALU.subtract).then_inc(c_lo, 1)
                elif kind in "qk":
                    i = 2 * n + (kind == "k")
                    pool.wait_ge(qk_mul, i + 1)
                    pool.tensor_tensor(rot1[:, i % 2, :, :], rot1[:, i % 2, :, :],
                                       rot2[:, i % 2, :, :], ALU.add).then_inc(qk_add, 1)
                elif kind == "stat":
                    pool.wait_ge(ln_stat, n + 1)
                    link(pool.tensor_scalar(vare[:, :], mv[:, :, 1], EPS, None, ALU.add))
                    pool.tensor_tensor(rstd[:, :], vare[:, :], mhalf[:, :],
                                       ALU.pow).then_inc(ln_rstd, 1)

            for job in jobs_a + [j for n in range(N + 2) for j in after[n]]:
                do(job)

        @block.scalar
        def _(act):
            act.wait_ge(in_const, consts)
            act.activation(tg[:, :], gates_in[:, :], ACT.Tanh).then_inc(tg_done, 1)
            act.activation(rwh[:, :, :], rw[:, :, :], ACT.Copy).then_inc(rw_hi, 1)

            def round_bank_pair(dst, job, ready, done):
                act.wait_ge(ready, job[1] + 1)
                two = banks(job)
                if job in ring_at:
                    act.activation(dst[:, :, :], both_banks(job)[:, :, :], ACT.Copy).then_inc(done, 1)
                else:
                    act.activation(dst[:, 0, :], two[0], ACT.Copy)
                    act.activation(dst[:, 1, :], two[1], ACT.Copy).then_inc(done, 1)

            def do(job):
                kind, n = job
                if kind == "w":
                    act.wait_ge(in_raw[n % RAW], 16 * (n // RAW + 1))
                    wait_slot_free(act, n)
                    act.activation(wh[:, slot(n), :], raw[:, n % RAW, :], ACT.Copy).then_inc(w_hi, 1)
                elif kind == "ctx":
                    act.wait_ge(in_ctx, 16 * (n + 1))
                    if n:
                        act.wait_ge(v_pe, GROUPS * n)
                    act.activation(xTh[1][:, :, :], craw[:, :, :], ACT.Copy).then_inc(c_hi, 1)
                elif kind == "xT":
                    round_bank_pair(xTh[side(n)], job, xT_pe, xT_hi)
                elif kind == "v":
                    act.wait_ge(v_pe, n + 1)
                    if n >= 2:
                        act.wait_ge(o_pe, G * (n - 1))
                        act.wait_ge(v_in[n % 2], 32 * (fillings(n) - 1))
                    act.activation(v_al[:, n % 2, :, :].rearrange("p t d -> p (t d)"),
                                   both_banks(job)[:, :, :].rearrange("p a n -> p (a n)"),
                                   ACT.Copy).then_inc(v_out, 1)
                elif kind == "oT":
                    if n:
                        act.wait_ge(y_pe, n)
                    round_bank_pair(oTh, job, oT_pe, oT_hi)
                elif kind == "r":
                    act.wait_ge(r_sub, n + 1)
                    act.activation(lexp[:, :, :], lex[:, :, :], ACT.Exp).then_inc(r_exp, 1)

            def softmax_numerator(c):
                act.wait_ge(s_max, c + 1)
                if c >= 2:
                    act.wait_ge(p_pe, c - 1)
                for t in range(TT):
                    last = act.activation(prob[:, c % 2, t, :], sneg[:, c % 2, t, :], ACT.Exp,
                                          bias=nmax[:, c % 4, t:t + 1], scale=-1.0,
                                          accum_out=rsum[:, c % 4, t:t + 1])
                last.then_inc(s_exp, 1)

            def copy_transposed(c):
                act.wait_ge(p_pe, c + 1)
                if c >= 2:
                    act.wait_ge(o_pe, c - 1)
                act.activation(pT[:, c % 2, :, :], psT[:, :, :], ACT.Copy).then_inc(p_out, 1)

            for job in prologue:
                do(job)
            for c, jobs in steps:
                if 1 <= c <= CHUNKS:
                    copy_transposed(c - 1)
                if c < CHUNKS:
                    softmax_numerator(c)
                for job in jobs:
                    do(job)

            def gelu(n):
                act.wait_ge(up_pe, n + 1)
                if n >= 2:
                    act.wait_ge(f_lo, n - 1)
                act.activation(act_g[:, n % 2, :], ring[(n // 2) % 2][:, n % 2, :],
                               ACT.Gelu).then_inc(f_gelu, 1)

            def round_gated(n):
                b, e = experts[n]
                if e < NS:
                    act.wait_ge(f_gelu, n + 1)
                else:
                    act.wait_ge(f_mul, b * NR + e - NS + 1)
                if n < 2:
                    act.wait_ge(y_pe, UNITS)
                else:
                    act.wait_ge(down_pe, n - 1)
                src = act_g if e < NS else act_f
                act.activation(oTh[:, n % 2, :], src[:, n % 2, :], ACT.Copy).then_inc(f_hi, 1)

            for n in range(N + 2):
                if n < N:
                    gelu(n)
                if 1 <= n <= N:
                    round_gated(n - 1)
                for job in after[n]:
                    do(job)

        @block.vector
        def _(dve):
            links = [0]

            def link(ins):
                links[0] += 1
                ins.then_inc(dve_link, 1)
                dve.wait_ge(dve_link, links[0])

            def rest_bank_pair(dst, hi, job, hi_done, done):
                dve.wait_ge(hi_done, job[1] + 1)
                two = banks(job)
                if job in ring_at:
                    dve.tensor_tensor(dst[:, :, :], both_banks(job)[:, :, :], hi[:, :, :].bitcast(F32),
                                      ALU.subtract).then_inc(done, 1)
                else:
                    dve.tensor_tensor(dst[:, 0, :], two[0], hi[:, 0, :].bitcast(F32), ALU.subtract)
                    dve.tensor_tensor(dst[:, 1, :], two[1], hi[:, 1, :].bitcast(F32),
                                      ALU.subtract).then_inc(done, 1)

            def statistics(j):
                b = j % B
                if j < B:
                    dve.wait_ge(in_x[b], 16)
                else:
                    dve.wait_ge(y_out, GROUPS * (b + 1))
                for t in range(TT):
                    last = dve.bn_stats(stats[:, t, :], x[:, b, t, :])
                link(last)
                for t in range(TT):
                    last = dve.bn_aggr(mv[:, t, :], stats[:, t, :])
                last.then_inc(ln_stat, 1)

            def normalise(j):
                dve.wait_ge(ln_rstd, j + 1)
                if j:
                    dve.wait_ge(xT_pe, j)
                for t in range(TT):
                    last = dve.tensor_scalar(xn[:, t, :], x[:, j % B, t, :], mv[:, t, 0:1],
                                             rstd[:, t:t + 1], ALU.subtract, ALU.mult)
                last.then_inc(ln_norm, 1)

            def rotate(job):
                kind, u = job
                i = 2 * u + (kind == "k")
                dve.wait_ge(qk_pe, i + 1)
                if i < 2:
                    dve.wait_ge(in_const, consts)
                else:
                    dve.wait_ge((k_in if kind == "k" else q_in)[(u - 1) % 2],
                                16 * 2 * G * fillings(u - 1))
                both = both_banks(job)
                dve.tensor_tensor(rot1[:, i % 2, :, :], both[:, :, :],
                                  cos[:, :].unsqueeze(1).to_broadcast([P, 2, L]), ALU.mult)
                dve.tensor_tensor(rot2[:, i % 2, :, :], both[:, ::-1, :], sin[:, :, :],
                                  ALU.mult).then_inc(qk_mul, 1)

            def router(b):
                job = ("r", b)
                logits = banks(job)[0][:, 0:TT * NR].rearrange("p (t e) -> p t e", t=TT)
                dve.wait_ge(r_pe, b + 1)
                link(dve.tensor_reduce(lmax[:, :], logits, AX_X, ALU.max))
                dve.tensor_tensor(lex[:, :, :], logits,
                                  lmax[:, :].unsqueeze(2).to_broadcast([P, TT, NR]),
                                  ALU.subtract).then_inc(r_sub, 1)
                dve.wait_ge(r_exp, b + 1)
                link(dve.tensor_reduce(lsum[:, :], lexp[:, :, :], AX_X, ALU.add))
                link(dve.reciprocal(linv[:, :], lsum[:, :]))
                if b == 0:
                    dve.wait_ge(pool_init, 1)
                link(dve.tensor_tensor(pr[:, :, 0:NR], lexp[:, :, :],
                                       linv[:, :].unsqueeze(2).to_broadcast([P, TT, NR]), ALU.mult))
                for t in range(TT):
                    last = dve.max(top[:, t, :], pr[:, t, 0:NR])
                link(last)
                link(dve.memset(top[:, :, TOPK:8], -1.0))
                for t in range(TT):
                    last = dve.match_replace(rep[:, t, :], top[:, t, :], pr[:, t, :], -2.0)
                link(last)
                if b:
                    dve.wait_ge(gT_pe, b)
                dve.scalar_tensor_tensor(gate[:, :, :], rep[:, :, 0:NR], -1.5, pr[:, :, 0:NR],
                                         ALU.is_lt, ALU.mult).then_inc(r_gate, 1)

            def do(job):
                kind, n = job
                if kind == "w" and n < 3:
                    dve.wait_ge(w_hi, n + 1)
                    dve.tensor_tensor(wl[:, slot(n), :], raw[:, n % RAW, :],
                                      wh[:, slot(n), :].bitcast(F32), ALU.subtract
                                      ).then_inc(w_lo_v, 1)
                elif kind == "stat":
                    statistics(n)
                elif kind == "norm":
                    normalise(n)
                elif kind == "xT":
                    rest_bank_pair(xTl[side(n)], xTh[side(n)], job, xT_hi, xT_lo)
                elif kind in "qk":
                    rotate(job)
                elif kind == "oT":
                    rest_bank_pair(oTl, oTh, job, oT_hi, oT_lo)
                elif kind == "y":
                    b = n // GROUPS
                    dve.wait_ge(y_pe, n + 1)
                    if n:
                        dve.wait_ge(y_out, n)
                    else:
                        dve.wait_ge(tg_done, 1)
                    dve.scalar_tensor_tensor(x[:, b, :, :].rearrange("p t d -> p (t d)"),
                                             both_banks(job)[:, :, :].rearrange("p a n -> p (a n)"),
                                             tg[:, 0:1], x[:, b, :, :].rearrange("p t d -> p (t d)"),
                                             ALU.mult, ALU.add).then_inc(y_out, 1)
                elif kind == "r":
                    router(n)
                elif kind == "gT":
                    dve.wait_ge(gT_pe, n + 1)
                    if n:
                        dve.wait_ge(gT_dram, 16 * n)
                    dve.tensor_copy(gT, banks(job)[0][0:NR, :]).then_inc(gT_out, 1)
                elif kind == "z":
                    dve.wait_ge(down_pe, NE * (n + 1))
                    for i in range(2):
                        last = dve.scalar_tensor_tensor(
                            x[:, n, 2 * i:2 * i + 2, :].rearrange("p t d -> p (t d)"),
                            psS[i][:, :, :].rearrange("p t c -> p (t c)"), tg[:, 1:2],
                            x[:, n, 2 * i:2 * i + 2, :].rearrange("p t d -> p (t d)"),
                            ALU.mult, ALU.add)
                    last.then_inc(z_out, 1)

            def score_max(c):
                dve.wait_ge(s_pe, c + 1)
                if c >= 2:
                    dve.wait_ge(s_exp, c - 1)
                for t in range(TT):
                    last = dve.tensor_tensor_reduce(sneg[:, c % 2, t, :], psS[c % 2][:, t, :],
                                                    mask[:, min(t, 1), :], -SCALE, -MASKED * 1e3,
                                                    ALU.add, ALU.min, nmax[:, c % 4, t:t + 1])
                last.then_inc(s_max, 1)

            def divide(pair):
                u, pp = divmod(pair, 2)
                c = 2 * pair
                dve.wait_ge(s_exp, c + 2)
                if pair:
                    dve.wait_ge(o_out, pair)
                dve.reciprocal(rinv[:, :, :], rsum[:, c % 4:c % 4 + 2, :]).then_inc(o_inv, 1)
                dve.wait_ge(o_pe, c + 2)
                dve.wait_ge(o_inv, pair + 1)
                if u >= 2:
                    dve.wait_ge(oT_pe, u - 1)
                for h in range(2):
                    at = (2 * pp + h) * DH
                    last = dve.tensor_tensor(att[:, u % 2, :, at:at + DH], psO[:, h, :, :],
                                             rinv[:, h, :].unsqueeze(2).to_broadcast([P, TT, DH]),
                                             ALU.mult)
                last.then_inc(o_out, 1)

            dve.wait_ge(rw_hi, 1)
            dve.tensor_tensor(rwl[:, :, :], rw[:, :, :], rwh[:, :, :].bitcast(F32),
                              ALU.subtract).then_inc(rw_lo, 1)
            for job in prologue:
                do(job)
            for c, jobs in steps:
                if c < CHUNKS:
                    score_max(c)
                if c >= 3 and c % 2 and c - 2 < CHUNKS:
                    divide((c - 2) // 2)
                for job in jobs:
                    do(job)

            def gated(n):
                b, e = experts[n]
                r = e - NS
                dve.wait_ge(f_gelu, n + 1)
                dve.wait_ge(gate_in[r], 16 * (b + 1))
                dve.wait_ge(f_hi, n - 1)
                dve.tensor_tensor(act_f[:, n % 2, :], act_g[:, n % 2, :], gate_bc[:, r, :],
                                  ALU.mult).then_inc(f_mul, 1)

            def rest_gated(n):
                b, e = experts[n]
                dve.wait_ge(f_hi, n + 1)
                src = act_g if e < NS else act_f
                dve.tensor_tensor(oTl[:, n % 2, :], src[:, n % 2, :], oTh[:, n % 2, :].bitcast(F32),
                                  ALU.subtract).then_inc(f_lo, 1)

            for n in range(N + 2):
                if n < N and experts[n][1] >= NS:
                    gated(n)
                if 1 <= n <= N:
                    rest_gated(n - 1)
                for job in after[n]:
                    do(job)

        @block.tensor
        def _(pe):
            def product(out, stationary, moving, start=True, stop=True, check=False):
                n = len(stationary)
                for i, (s, m) in enumerate(zip(stationary, moving)):
                    for j, (a, b) in enumerate(products(s, m)):
                        last = pe.matmul(out, a, b, start=start and i == 0 and j == 0,
                                         stop=stop and i == n - 1 and j == 2,
                                         skip_group_check=check)
                return last

            def weights(i):
                pe.wait_ge(w_hi, i + 1)
                wait_w_lo(pe, i)

            def cols(i, a, n):
                return wh[:, slot(i), a:a + n], wl[:, slot(i), a:a + n]

            def claim(job):
                if job in ring_at:
                    if ring_at[job] >= 2:
                        pe.wait_ge(*released(ring_jobs[ring_at[job] - 2]))
                elif job[0] == "xT":
                    pe.wait_ge(p_out, CHUNKS)
                    pe.wait_ge(o_out, CHUNKS // 2)
                    if job[1] > B + 1:
                        pe.wait_ge(gT_out, job[1] - B)
                elif job[0] == "r":
                    pe.wait_ge(xT_lo, B + job[1] + 1)
                elif job[0] == "gT":
                    pe.wait_ge(r_sub, job[1] + 1)

            def do(job):
                kind, n = job
                if kind not in in_ring:
                    return
                claim(job)
                two = banks(job)
                if kind == "xT":
                    if n == 0:
                        pe.wait_ge(in_const, consts)
                    pe.wait_ge(ln_norm, n + 1)
                    for kc in range(KC):
                        for t in range(TT):
                            last = pe.transpose(two[kc][:, t * P:(t + 1) * P],
                                                xn[:, t, kc * P:(kc + 1) * P], ident[:, :])
                    last.then_inc(xT_pe, 1)
                elif kind in "qk":
                    b, g = divmod(n, GROUPS)
                    i = 4 * g + (kind == "k")
                    weights(i)
                    if kind == "q":
                        pe.wait_ge(xT_lo, b + 1)
                    else:
                        pe.wait_ge(c_lo, b + 1)
                    X = 0 if kind == "q" else 1
                    for half in range(2):
                        last = product(two[half], [cols(i, kc * D + half * P, P) for kc in range(KC)],
                                       [(xTh[X][:, kc, :], xTl[X][:, kc, :]) for kc in range(KC)])
                    last.then_inc(qk_pe, 1)
                elif kind == "v":
                    b, g = divmod(n, GROUPS)
                    i = 4 * g + 2
                    weights(i)
                    pe.wait_ge(c_lo, b + 1)
                    for t in range(TT):
                        last = product(two[t // 2][:, (t % 2) * GD:(t % 2 + 1) * GD],
                                       [(xTh[1][:, kc, t * P:(t + 1) * P],
                                         xTl[1][:, kc, t * P:(t + 1) * P]) for kc in range(KC)],
                                       [cols(i, kc * D, D) for kc in range(KC)])
                    last.then_inc(v_pe, 1)
                elif kind == "oT":
                    pe.wait_ge(o_out, 2 * (n + 1))
                    for j in range(2):
                        for t in range(TT):
                            last = pe.transpose(two[j][:, t * P:(t + 1) * P],
                                                att[:, n % 2, t, j * P:(j + 1) * P], ident[:, :])
                    last.then_inc(oT_pe, 1)
                elif kind == "y":
                    i = 4 * (n % GROUPS) + 3
                    weights(i)
                    pe.wait_ge(oT_lo, n + 1)
                    for t in range(TT):
                        last = product(two[t // 2][:, (t % 2) * D:(t % 2 + 1) * D],
                                       [(oTh[:, j, t * P:(t + 1) * P], oTl[:, j, t * P:(t + 1) * P])
                                        for j in range(2)],
                                       [cols(i, j * D, D) for j in range(2)])
                    last.then_inc(y_pe, 1)
                elif kind == "r":
                    pe.wait_ge(rw_lo, 1)
                    pe.wait_ge(xT_lo, B + n + 1)
                    X = side(B + n)
                    for t in range(TT):
                        last = product(two[0][:, t * NR:(t + 1) * NR],
                                       [(xTh[X][:, kc, t * P:(t + 1) * P],
                                         xTl[X][:, kc, t * P:(t + 1) * P]) for kc in range(KC)],
                                       [(rwh[:, kc, :], rwl[:, kc, :]) for kc in range(KC)])
                    last.then_inc(r_pe, 1)
                elif kind == "gT":
                    pe.wait_ge(r_gate, n + 1)
                    for t in range(TT):
                        last = pe.transpose(two[0][0:NR, t * P:(t + 1) * P], gate[:, t, :], ident[:, :])
                    last.then_inc(gT_pe, 1)

            def scores(c):
                u, h = divmod(c, G)
                rows = slice((h % 2) * DH, (h % 2) * DH + DH)
                if h == 0:
                    pe.wait_ge(q_in[u % 2], 16 * 2 * G * fillings(u))
                    pe.wait_ge(k_in[u % 2], 16 * 2 * G * fillings(u))
                if c >= 2:
                    pe.wait_ge(s_max, c - 1)
                for blk in range(L // W):
                    t, e = divmod(blk, 2)
                    last = pe.matmul(psS[c % 2][e * W:(e + 1) * W, t, :],
                                     qT[rows, u % 2, h // 2, blk * W:(blk + 1) * W],
                                     kT[rows, u % 2, h // 2, blk * W:(blk + 2) * W],
                                     start=True, stop=True)
                last.then_inc(s_pe, 1)

            def transpose_probs(c):
                pe.wait_ge(s_exp, c + 1)
                if c:
                    pe.wait_ge(p_out, c)
                for t in range(TT):
                    last = pe.transpose(psT[:, t, :], prob[:, c % 2, t, :], ident[:, :])
                last.then_inc(p_pe, 1)

            def values(c):
                u, h = divmod(c, G)
                pe.wait_ge(p_out, c + 1)
                if h == 0:
                    pe.wait_ge(v_out, u + 1)
                    pe.wait_ge(v_in[u % 2], 32 * fillings(u))
                if c == 0:
                    pe.wait_ge(pool_init, 1)
                if c % 2 == 0 and c:
                    pe.wait_ge(o_out, c // 2)
                for blk in range(L // W):
                    t, e = divmod(blk, 2)
                    v = v_al if e else v_sh
                    last = pe.matmul(psO[e * W:(e + 1) * W, c % 2, t, :],
                                     pT[:, c % 2, t, e * W:(e + 1) * W],
                                     v[:, u % 2, t, h * DH:(h + 1) * DH], start=True, stop=True)
                last.then_inc(o_pe, 1)

            for job in prologue:
                do(job)
            for c, jobs in steps:
                if c < CHUNKS:
                    scores(c)
                if 1 <= c <= CHUNKS:
                    transpose_probs(c - 1)
                if 2 <= c <= CHUNKS + 1:
                    values(c - 2)
                for job in jobs:
                    do(job)

            def up(n):
                b, e = experts[n]
                i = expert_piece(e)
                if b == 0:
                    weights(i)
                if n < 4:
                    pe.wait_ge(*released(ring_jobs[-1]))
                    pe.wait_ge(*released(ring_jobs[-2]))
                else:
                    pe.wait_ge(f_gelu, n - 3)
                if e == 0:
                    pe.wait_ge(xT_lo, B + b + 1)
                X = side(B + b)
                product(ring[(n // 2) % 2][:, n % 2, :], [cols(i, kc * P, P) for kc in range(KC)],
                        [(xTh[X][:, kc, :], xTl[X][:, kc, :]) for kc in range(KC)]
                        ).then_inc(up_pe, 1)

            def down(n):
                b, e = experts[n]
                i = expert_piece(e)
                pe.wait_ge(f_lo, n + 1)
                if e == 0:
                    if b:
                        pe.wait_ge(z_out, b)
                    else:
                        pe.wait_ge(s_max, CHUNKS)
                for t in range(TT):
                    last = product(psS[t // 2][:, 2 * (t % 2):2 * (t % 2) + 2, :].rearrange("p a c -> p (a c)"),
                                   [(oTh[:, n % 2, t * P:(t + 1) * P], oTl[:, n % 2, t * P:(t + 1) * P])],
                                   [cols(i, D, D)], start=(e == 0 and t % 2 == 0), stop=(e == NE - 1),
                                   check=True)
                last.then_inc(down_pe, 1)

            for n in range(N + 2):
                if n < N:
                    up(n)
                if n >= 2:
                    down(n - 2)
                for job in after[n]:
                    do(job)


_OUT = ((B, L, D), "float32")


def tables():
    freqs = (1.0 / np.float32(ROPE_BASE) ** (np.arange(0, DH, 2, dtype=np.float32) / np.float32(DH)))
    ang = np.arange(L, dtype=np.float32)[:, None] * freqs.astype(np.float32)[None, :]
    cos, sin = (np.ascontiguousarray(np.tile(f(ang).astype(np.float32).T, (G, 1))) for f in (np.cos, np.sin))
    r = np.arange(P)[:, None] % W
    c = np.arange(P)[None, :]
    seen = np.where(c < W, c >= r, c - W <= r)
    first = seen & ~((np.arange(P)[:, None] < W) & (c < W))
    mask = np.stack([np.where(m, 0.0, MASKED) for m in (first, seen)], 1).astype(np.float32)
    return cos, np.ascontiguousarray(np.stack([-sin, sin], 1)), mask, np.eye(P, dtype=np.float32)


def kernel(x, ctx_1024, g_xattn, g_ffn, L0_xattn_wq, L0_xattn_wk, L0_xattn_wv, L0_xattn_wo,
           L0_ffn_shared_up, L0_ffn_shared_down, L0_ffn_routed_up, L0_ffn_routed_down,
           L0_ffn_router_w):
    import concourse.bacc as bacc
    from concourse.bass_utils import run_bass_kernel_spmd

    def a(v):
        return np.asarray(v)

    xt = a(x).reshape(B, TT, P, D).transpose(0, 2, 1, 3)
    ct = a(ctx_1024).reshape(B, L, KC, P).transpose(0, 3, 2, 1)
    wq, wk = (a(w).reshape(GROUPS, G, HALF, 2, KC, P).transpose(0, 5, 4, 3, 1, 2).reshape(GROUPS, P, PIECE)
              for w in (L0_xattn_wq, L0_xattn_wk))
    wv = a(L0_xattn_wv).reshape(GROUPS, GD, KC, P).transpose(0, 3, 2, 1).reshape(GROUPS, P, PIECE)
    wo = a(L0_xattn_wo).reshape(D, GROUPS, 2, P).transpose(1, 3, 2, 0).reshape(GROUPS, P, PIECE)
    w = np.stack([wq, wk, wv, wo], 1).reshape(WPIECES, P, PIECE)
    up = np.concatenate([a(L0_ffn_shared_up), a(L0_ffn_routed_up)]).reshape(NE, P, KC, P)
    up = up.transpose(0, 3, 2, 1).reshape(NE, P, D)
    down = np.concatenate([a(L0_ffn_shared_down), a(L0_ffn_routed_down)]).transpose(0, 2, 1)
    e = np.concatenate([up, down], 2)
    rw = a(L0_ffn_router_w).reshape(NR, KC, P).transpose(2, 1, 0)
    cos, sin, mask, ident = tables()
    arrays = dict(x=xt, ctx=ct, gx=a(g_xattn), gf=a(g_ffn), w=w, e=e, rw=rw, cos=cos, sin=sin,
                  mask=mask, ident=ident)
    arrays = {f"in_{k}": np.ascontiguousarray(v) for k, v in arrays.items()}
    nc = bacc.Bacc("TRN2", target_bir_lowering=False, num_devices=1)
    args = [nc.dram_tensor(k, v.shape, F32, kind="ExternalInput").ap() for k, v in arrays.items()]
    args.append(nc.dram_tensor("out", (B, P, TT, D), F32, kind="ExternalOutput").ap())
    build(nc, *args)
    got = run_bass_kernel_spmd(nc, [arrays], core_ids=[0]).results[0]["out"]
    return np.asarray(got).reshape(B, P, TT, D).transpose(0, 2, 1, 3).reshape(B, L, D)
```

```python
from contextlib import ExitStack

import numpy as np

from concourse import mybir

F32 = mybir.dt.float32
F32R = mybir.dt.float32r
ALU = mybir.AluOpType
ACT = mybir.ActivationFunctionType
AX_X = mybir.AxisListType.X

P = 128
B, L, D = 4, 512, 256
H, DH, W = 16, 64, 64
QUAD = 32
ROPE_BASE = 10000.0
KC = D // P
TT = L // P
G = 4
GD = G * DH
GROUPS = H // G
UNITS = B * GROUPS
CHUNKS = UNITS * G
NS, NR, TOPK = 2, 16, 4
NE = NS + NR
SENT = 8 - TOPK
EPS = 1e-5
SCALE = float(DH) ** -0.5
MASKED = -1e30
PIECE = KC * D
WPIECES = 4 * GROUPS
RAW = 4


def products(stationary, moving):
    (sh, sl), (mh, ml) = stationary, moving
    return ((sh, mh), (sh, ml), (sl, mh))


def build(nc, x_d, ctx_d, gx_d, gf_d, w_d, e_d, rw_d, cos_d, sin_d, mask_d, ident_d, out_d):
    with ExitStack() as ctx:
        def sb(name, shape, dt=F32):
            return ctx.enter_context(nc.sbuf_tensor(name, shape, dt))

        def sem(name):
            return ctx.enter_context(nc.semaphore(name))

        x = sb("x", [P, B, TT, D])
        wh = sb("wh", [P, NE, PIECE], F32R)
        wl = sb("wl", [P, NE, PIECE], F32R)
        raw = sb("raw", [P, RAW, PIECE])
        xTh = [sb(f"xTh{i}", [P, KC, L], F32R) for i in range(2)]
        xTl = [sb(f"xTl{i}", [P, KC, L], F32R) for i in range(2)]
        craw = sb("craw", [P, KC, L])
        cos = sb("cos", [P, L])
        sin = sb("sin", [P, L])
        mask = sb("mask", [P, 2, P])
        ident = sb("ident", [P, P])
        xn = sb("xn", [P, TT, D])
        stats = sb("stats", [P, TT, 6])
        mv = sb("mv", [P, TT, 2])
        vare = sb("vare", [P, TT])
        rstd = sb("rstd", [P, TT])
        mhalf = sb("mhalf", [P, TT])
        gates_in = sb("gates_in", [P, 2])
        tg = sb("tg", [P, 2])
        rw = sb("rw", [P, KC, NR])
        rwh = sb("rwh", [P, KC, NR], F32R)
        rwl = sb("rwl", [P, KC, NR], F32R)
        sizes = dict(swap=(2, 2, L), qT=(2, 2, L), kT=(2, 2, W + L), spare=(1, 2, 896),
                     v_al=(2, TT, GD), v_sh=(2, TT, GD))
        arena = sb("arena", [P, sum(int(np.prod(s)) for s in sizes.values())])
        cuts, at = {}, 0
        for name, (a, b, c) in sizes.items():
            cuts[name] = arena[:, at:at + a * b * c].rearrange("p (a b c) -> p a b c", a=a, b=b)
            at += a * b * c
        swap = cuts["swap"]
        qT, kT = cuts["qT"], cuts["kT"]
        v_al, v_sh = cuts["v_al"], cuts["v_sh"]
        gate_bc = arena[:, 0:NR * L].rearrange("p (e n) -> p e n", e=NR)
        sneg = sb("sneg", [P, 2, TT, P])
        prob = sb("prob", [P, 3, TT, P])
        pT = sb("pT", [P, 4, TT, P])
        nmax = sb("nmax", [P, 4, TT])
        rsum = sb("rsum", [P, 4, TT])
        rinv = sb("rinv", [P, 2, TT])
        oTh = sb("oTh", [P, 2, L], F32R)
        oTl = sb("oTl", [P, 2, L], F32R)
        act_g = sneg[:, :, :, :].rearrange("p a t c -> p a (t c)")
        act_f = prob[:, :, :, :].rearrange("p a t c -> p a (t c)")
        lmax = sb("lmax", [P, TT])
        lex = sb("lex", [P, TT, NR])
        lexp = sb("lexp", [P, TT, NR])
        lsum = sb("lsum", [P, TT])
        linv = sb("linv", [P, TT])
        pr = sb("pr", [P, TT, NR + SENT])
        top = sb("top", [P, TT, 8])
        rep = sb("rep", [P, TT, NR + SENT])
        gate = sb("gate", [P, TT, NR])
        gT = craw[0:NR, 0, :]
        gT_d = nc.dram_tensor("gate_scratch", (B, NR, L), F32).ap()

        ring = [ctx.enter_context(nc.psum_tensor(f"ring{i}", [P, 2, L], F32)) for i in range(2)]
        psS = [ctx.enter_context(nc.psum_tensor(f"psS{i}", [P, TT, P], F32)) for i in range(2)]
        psT = ctx.enter_context(nc.psum_tensor("psT", [P, TT, P], F32))
        psO = ctx.enter_context(nc.psum_tensor("psO", [P, L], F32))

        in_x = [sem(f"in_x{b}") for b in range(B)]
        in_ctx = sem("in_ctx")
        in_raw = [sem(f"in_raw{i}") for i in range(RAW)]
        in_ident, in_rope = sem("in_ident"), sem("in_rope")
        in_const = sem("in_const")
        pool_init = sem("pool_init")
        w_hi = sem("w_hi")
        w_lo_v = sem("w_lo_v")
        w_lo_p = sem("w_lo_p")
        rw_hi, rw_lo = sem("rw_hi"), sem("rw_lo")
        c_hi, c_lo = sem("c_hi"), sem("c_lo")
        tg_done = sem("tg_done")
        ln_stat = sem("ln_stat")
        ln_rstd = sem("ln_rstd")
        ln_norm = sem("ln_norm")
        xT_pe, xT_hi, xT_lo = sem("xT_pe"), sem("xT_hi"), sem("xT_lo")
        qk_pe = [sem("q_pe"), sem("k_pe")]
        qk_swap = [sem("q_swap"), sem("k_swap")]
        qk_mul = [sem("q_mul"), sem("k_mul")]
        qk_rot = [sem("q_rot"), sem("k_rot")]
        v_pe, v_out = sem("v_pe"), sem("v_out")
        v_in = [sem(f"v_in{i}") for i in range(2)]
        s_pe, s_max, s_exp = sem("s_pe"), sem("s_max"), sem("s_exp")
        s_inv, s_norm = sem("s_inv"), sem("s_norm")
        p_pe, p_out = sem("p_pe"), sem("p_out")
        oT_pe, oT_hi, oT_lo = sem("oT_pe"), sem("oT_hi"), sem("oT_lo")
        y_pe, y_out = sem("y_pe"), sem("y_out")
        dve_link, pool_link = sem("dve_link"), sem("pool_link")
        r_pe, r_sub, r_exp, r_gate = sem("r_pe"), sem("r_sub"), sem("r_exp"), sem("r_gate")
        gT_pe, gT_out, gT_dram = sem("gT_pe"), sem("gT_out"), sem("gT_dram")
        gate_in = [sem(f"gate_in{i}") for i in range(NR)]
        up_pe, f_gelu, f_mul = sem("up_pe"), sem("f_gelu"), sem("f_mul")
        f_hi, f_lo, down_pe = sem("f_hi"), sem("f_lo"), sem("down_pe")
        z_out, out_done = sem("z_out"), sem("out_done")

        def slot(i):
            return i if i < NE else i - NE

        def expert_piece(e):
            return WPIECES + e

        prologue = [("ctx", 0), ("w", 0), ("w", 1), ("stat", 0), ("norm", 0), ("k", 0), ("w", 2),
                    ("xT", 0), ("v", 0), ("q", 0), ("w", 3), ("w", 4), ("w", 5), ("k", 1), ("v", 1),
                    ("w", 6), ("w", 7)]
        steps = []
        for c in range(CHUNKS + 4):
            u, k = divmod(c, 4)
            b, g = divmod(u, GROUPS)
            jobs = []
            if k == 0 and u + 1 < UNITS:
                jobs.append(("q", u + 1))
            if k == 1 and 1 <= u and u + 1 < UNITS:
                jobs.append(("k", u + 1))
            if k == 1 and g == 2 and b + 1 < B:
                jobs.append(("xT", b + 1))
            if k == 2 and 1 <= u and u + 1 < UNITS:
                jobs.append(("v", u + 1))
            if k == 3 and u >= 1:
                jobs.append(("y", u - 1))
            if k == 3 and g == 2 and b + 1 < B:
                jobs.append(("ctx", b + 1))
            if u < 2 and k >= 2:
                jobs += [("w", 8 + 4 * u + 2 * (k - 2)), ("w", 9 + 4 * u + 2 * (k - 2))]
            if k == 3 and g == 1 and b + 1 < B:
                jobs.append(("stat", b + 1))
            if k == 0 and g == 2 and b + 1 < B:
                jobs.append(("norm", b + 1))
            jobs += {(UNITS - 3, 1): [("stat", B)], (UNITS - 3, 3): [("norm", B)],
                     (UNITS - 2, 1): [("xT", B)], (UNITS - 2, 2): [("r", 0)],
                     (UNITS - 1, 0): [("gT", 0)]}.get((u, k), [])
            if (u, k) == (UNITS - 4, 0):
                jobs += [("w", expert_piece(e)) for e in range(NS)]
            if k == 0 and u >= UNITS - 2:
                first = NS + 4 * (u - (UNITS - 2))
                jobs += [("w", expert_piece(e)) for e in range(first, first + 4)]
            steps.append((c, jobs))
        attended = {2 * p + 4: p for p in range(CHUNKS // 2)}
        experts = [(b, e) for b in range(B) for e in range(NE)]
        N = len(experts)
        after = {n: [] for n in range(N + 2)}
        after[0] += [("w", expert_piece(e)) for e in range(NE - 4, NE)]
        for b in range(B - 1):
            for e, kind in ((1, "stat"), (2, "norm"), (4, "xT"), (7, "r"), (10, "gT")):
                after[b * NE + e].append((kind, b + 1 + (B if kind in ("stat", "norm", "xT") else 0)))
        for b in range(B):
            after[b * NE + NE + 1].append(("z", b))

        in_ring = ("xT", "q", "k", "v", "y", "r", "gT")
        jobs_a = [j for jobs in [prologue] + [jobs for _, jobs in steps] for j in jobs]
        ring_jobs = [j for j in jobs_a if j[0] in in_ring]
        ring_at = {j: n for n, j in enumerate(ring_jobs)}

        def banks(job):
            if job in ring_at:
                r = ring[ring_at[job] % 2]
                return [r[:, 0, :], r[:, 1, :]]
            return [psT[:, :, :].rearrange("p t c -> p (t c)"),
                    psO[:, :]]

        def both_banks(job):
            return ring[ring_at[job] % 2]

        def released(job):
            kind, n = job
            return {"xT": (xT_lo, n + 1), "q": (qk_mul[0], n + 1), "k": (qk_mul[1], n + 1),
                    "v": (v_out, n + 1), "y": (y_out, n + 1),
                    "r": (r_sub, n + 1), "gT": (gT_out, n + 1)}[kind]

        def fillings(u):
            return u // 2 + 1

        def side(j):
            return 0 if j < B else (j - B) % 2

        def wait_w_lo(eng, i):
            if i < 3:
                eng.wait_ge(w_lo_v, i + 1)
            else:
                eng.wait_ge(w_lo_p, i - 2)

        def wait_slot_free(eng, i):
            if i >= NE:
                g, m = divmod(slot(i), 4)
                eng.wait_ge(y_pe if m == 3 else v_pe, (B - 1) * GROUPS + g + 1)

        consts = 16 * 4
        block = ctx.enter_context(nc.Block())

        @block.sync
        def _(sp):
            def load_piece(i):
                if i >= RAW:
                    sp.wait_ge(w_hi, i - RAW + 1)
                    wait_w_lo(sp, i - RAW)
                src = w_d[i] if i < WPIECES else e_d[i - WPIECES]
                sp.dma_start(raw[:, i % RAW, :], src).then_inc(in_raw[i % RAW], 16)

            def load_ctx(b):
                if b:
                    sp.wait_ge(c_lo, b)
                sp.dma_start(craw[:, :, :], ctx_d[b]).then_inc(in_ctx, 16)

            def shift_values(u):
                sp.wait_ge(v_out, u + 1)
                sp.dma_start(v_sh[W:P, u % 2, :, :], v_al[0:W, u % 2, :, :]).then_inc(v_in[u % 2], 16)
                sp.dma_start(v_sh[0:W, u % 2, 1:TT, :],
                             v_al[W:P, u % 2, 0:TT - 1, :]).then_inc(v_in[u % 2], 16)

            def spread_gates(b):
                sp.wait_ge(gT_out, b + 1)
                sp.dma_start(gT_d[b], gT).then_inc(gT_dram, 16)
                sp.wait_ge(gT_dram, 16 * (b + 1))
                for r in range(NR):
                    if b:
                        sp.wait_ge(f_mul, (b - 1) * NR + r + 1)
                    elif r == 0:
                        sp.wait_ge(s_pe, CHUNKS)
                    sp.dma_start(gate_bc[:, r, :],
                                 gT_d[b, r].partition_broadcast(P)).then_inc(gate_in[r], 16)

            load_ctx(0)
            sp.dma_start(x[:, 0, :, :], x_d[0]).then_inc(in_x[0], 16)
            load_piece(0)
            sp.dma_start(ident[:, :], ident_d).then_inc(in_ident, 16)
            load_piece(1)
            load_piece(2)
            sp.dma_start(cos[:, :], cos_d).then_inc(in_rope, 16)
            sp.dma_start(sin[:, :], sin_d).then_inc(in_rope, 16)
            load_piece(3)
            for dst, src in ((mask[:, :, :], mask_d), (rw[:, :, :], rw_d),
                             (gates_in[:, 0:1], gx_d.partition_broadcast(P)),
                             (gates_in[:, 1:2], gf_d.partition_broadcast(P))):
                sp.dma_start(dst, src).then_inc(in_const, 16)
            for b in range(1, B):
                sp.dma_start(x[:, b, :, :], x_d[b]).then_inc(in_x[b], 16)

            def store(b):
                sp.wait_ge(z_out, b + 1)
                sp.dma_start(out_d[b], x[:, b, :, :]).then_inc(out_done, 16)

            def do(job):
                kind, n = job
                if kind == "w" and n + RAW < WPIECES + NE:
                    load_piece(n + RAW)
                elif kind == "ctx" and n + 1 < B:
                    load_ctx(n + 1)
                elif kind == "v":
                    shift_values(n)
                elif kind == "gT":
                    spread_gates(n)
                elif kind == "z":
                    store(n)

            for job in jobs_a + [j for n in range(N + 2) for j in after[n]]:
                do(job)
            sp.wait_ge(out_done, 16 * B)

        @block.gpsimd
        def _(pool):
            links = [0]

            def link(ins):
                links[0] += 1
                ins.then_inc(pool_link, 1)
                pool.wait_ge(pool_link, links[0])

            pool.memset(kT[:, :, :, 0:W], 0.0)
            pool.memset(v_sh[0:W, :, 0, :], 0.0)
            pool.memset(pr[:, :, NR:], -1.0)
            pool.memset(mhalf[:, :], -0.5).then_inc(pool_init, 1)
            pool.wait_ge(pool_init, 1)

            def do(job):
                kind, n = job
                if kind == "w" and n >= 3:
                    pool.wait_ge(w_hi, n + 1)
                    pool.tensor_tensor(wl[:, slot(n), :], raw[:, n % RAW, :],
                                       wh[:, slot(n), :].bitcast(F32),
                                       ALU.subtract).then_inc(w_lo_p, 1)
                elif kind == "ctx" and n:
                    pool.wait_ge(c_hi, n + 1)
                    pool.tensor_tensor(xTl[1][:, :, :], craw[:, :, :], xTh[1][:, :, :].bitcast(F32),
                                       ALU.subtract).then_inc(c_lo, 1)
                elif kind in "qk":
                    i = "qk".index(kind)
                    dst = qT[:, n % 2, :, :] if kind == "q" else kT[:, n % 2, :, W:]
                    if n == 0:
                        pool.wait_ge(in_rope, 32)
                    pool.wait_ge(qk_swap[i], n + 1)
                    link(pool.tensor_tensor(swap[:, i, :, :], swap[:, i, :, :],
                                            sin[:, :].unsqueeze(1).to_broadcast([P, 2, L]), ALU.mult))
                    pool.wait_ge(qk_mul[i], n + 1)
                    pool.tensor_tensor(dst, dst, swap[:, i, :, :], ALU.add).then_inc(qk_rot[i], 1)
                elif kind == "stat":
                    pool.wait_ge(ln_stat, n + 1)
                    link(pool.tensor_scalar(vare[:, :], mv[:, :, 1], EPS, None, ALU.add))
                    pool.tensor_tensor(rstd[:, :], vare[:, :], mhalf[:, :],
                                       ALU.pow).then_inc(ln_rstd, 1)

            for job in jobs_a + [j for n in range(N + 2) for j in after[n]]:
                do(job)

        @block.scalar
        def _(act):

            def round_bank_pair(dst, job, ready, done):
                act.wait_ge(ready, job[1] + 1)
                two = banks(job)
                if job in ring_at:
                    act.activation(dst[:, :, :], both_banks(job)[:, :, :], ACT.Copy).then_inc(done, 1)
                else:
                    act.activation(dst[:, 0, :], two[0], ACT.Copy)
                    act.activation(dst[:, 1, :], two[1], ACT.Copy).then_inc(done, 1)

            def do(job):
                kind, n = job
                if kind == "w":
                    act.wait_ge(in_raw[n % RAW], 16 * (n // RAW + 1))
                    wait_slot_free(act, n)
                    act.activation(wh[:, slot(n), :], raw[:, n % RAW, :], ACT.Copy).then_inc(w_hi, 1)
                elif kind == "ctx":
                    act.wait_ge(in_ctx, 16 * (n + 1))
                    if n:
                        act.wait_ge(v_pe, GROUPS * n)
                    act.activation(xTh[1][:, :, :], craw[:, :, :], ACT.Copy).then_inc(c_hi, 1)
                elif kind == "xT":
                    round_bank_pair(xTh[side(n)], job, xT_pe, xT_hi)
                elif kind == "v":
                    act.wait_ge(v_pe, n + 1)
                    if n >= 2:
                        act.wait_ge(oT_pe, 2 * (n - 1))
                        act.wait_ge(v_in[n % 2], 32 * (fillings(n) - 1))
                    act.activation(v_al[:, n % 2, :, :].rearrange("p t d -> p (t d)"),
                                   both_banks(job)[:, :, :].rearrange("p a n -> p (a n)"),
                                   ACT.Copy).then_inc(v_out, 1)
                elif kind == "r":
                    act.wait_ge(r_sub, n + 1)
                    act.activation(lexp[:, :, :], lex[:, :, :], ACT.Exp).then_inc(r_exp, 1)

            def softmax_numerator(c):
                act.wait_ge(s_max, c + 1)
                if c >= 3:
                    act.wait_ge(p_pe, c - 2)
                for t in range(TT):
                    last = act.activation(prob[:, c % 3, t, :], sneg[:, c % 2, t, :], ACT.Exp,
                                          bias=nmax[:, c % 4, t:t + 1], scale=-1.0,
                                          accum_out=rsum[:, c % 4, t:t + 1])
                last.then_inc(s_exp, 1)

            def copy_transposed(c):
                act.wait_ge(p_pe, c + 1)
                if c >= 4:
                    act.wait_ge(oT_pe, c // 2 - 1)
                act.activation(pT[:, c % 4, :, :], psT[:, :, :], ACT.Copy).then_inc(p_out, 1)

            def round_att(p):
                act.wait_ge(oT_pe, p + 1)
                if p >= 2:
                    act.wait_ge(y_pe, p // 2)
                act.activation(oTh[:, p % 2, :], psO[:, :], ACT.Copy).then_inc(oT_hi, 1)

            for job in prologue:
                do(job)
            act.wait_ge(in_const, consts)
            act.activation(tg[:, :], gates_in[:, :], ACT.Tanh).then_inc(tg_done, 1)
            act.activation(rwh[:, :, :], rw[:, :, :], ACT.Copy).then_inc(rw_hi, 1)
            for c, jobs in steps:
                if 3 <= c <= CHUNKS + 2:
                    copy_transposed(c - 3)
                if c < CHUNKS:
                    softmax_numerator(c)
                if c in attended:
                    round_att(attended[c])
                for job in jobs:
                    do(job)

            def gelu(n):
                act.wait_ge(up_pe, n + 1)
                if n >= 2:
                    act.wait_ge(f_lo, n - 1)
                act.activation(act_g[:, n % 2, :], ring[(n // 2) % 2][:, n % 2, :],
                               ACT.Gelu).then_inc(f_gelu, 1)

            def round_gated(n):
                b, e = experts[n]
                if e < NS:
                    act.wait_ge(f_gelu, n + 1)
                else:
                    act.wait_ge(f_mul, b * NR + e - NS + 1)
                if n < 2:
                    act.wait_ge(y_pe, UNITS)
                else:
                    act.wait_ge(down_pe, n - 1)
                src = act_g if e < NS else act_f
                act.activation(oTh[:, n % 2, :], src[:, n % 2, :], ACT.Copy).then_inc(f_hi, 1)

            for n in range(N + 2):
                if n < N:
                    gelu(n)
                if 1 <= n <= N:
                    round_gated(n - 1)
                for job in after[n]:
                    do(job)

        @block.vector
        def _(dve):
            links = [0]

            def link(ins):
                links[0] += 1
                ins.then_inc(dve_link, 1)
                dve.wait_ge(dve_link, links[0])

            def rest_bank_pair(dst, hi, job, hi_done, done):
                dve.wait_ge(hi_done, job[1] + 1)
                two = banks(job)
                if job in ring_at:
                    dve.tensor_tensor(dst[:, :, :], both_banks(job)[:, :, :], hi[:, :, :].bitcast(F32),
                                      ALU.subtract).then_inc(done, 1)
                else:
                    dve.tensor_tensor(dst[:, 0, :], two[0], hi[:, 0, :].bitcast(F32), ALU.subtract)
                    dve.tensor_tensor(dst[:, 1, :], two[1], hi[:, 1, :].bitcast(F32),
                                      ALU.subtract).then_inc(done, 1)

            def statistics(j):
                b = j % B
                if j < B:
                    dve.wait_ge(in_x[b], 16)
                else:
                    dve.wait_ge(y_out, GROUPS * (b + 1))
                for t in range(TT):
                    last = dve.bn_stats(stats[:, t, :], x[:, b, t, :])
                link(last)
                for t in range(TT):
                    last = dve.bn_aggr(mv[:, t, :], stats[:, t, :])
                last.then_inc(ln_stat, 1)

            def normalise(j):
                dve.wait_ge(ln_rstd, j + 1)
                if j:
                    dve.wait_ge(xT_pe, j)
                for t in range(TT):
                    last = dve.tensor_scalar(xn[:, t, :], x[:, j % B, t, :], mv[:, t, 0:1],
                                             rstd[:, t:t + 1], ALU.subtract, ALU.mult)
                last.then_inc(ln_norm, 1)

            def rotate(job):
                kind, u = job
                i = "qk".index(kind)
                dve.wait_ge(qk_pe[i], u + 1)
                if u:
                    dve.wait_ge(qk_rot[i], u)
                dve.stream_shuffle(swap[:, i, :, :], both_banks(job)[:, :, :],
                                   [(lane + QUAD // 2) % QUAD for lane in range(QUAD)]
                                   ).then_inc(qk_swap[i], 1)
                if u == 0:
                    dve.wait_ge(in_rope, 32)
                if u >= 2:
                    dve.wait_ge(s_pe, G * (u - 1))
                dst = qT[:, u % 2, :, :] if kind == "q" else kT[:, u % 2, :, W:]
                dve.tensor_tensor(dst, both_banks(job)[:, :, :],
                                  cos[:, :].unsqueeze(1).to_broadcast([P, 2, L]),
                                  ALU.mult).then_inc(qk_mul[i], 1)

            def router(b):
                job = ("r", b)
                logits = banks(job)[0][:, 0:TT * NR].rearrange("p (t e) -> p t e", t=TT)
                dve.wait_ge(r_pe, b + 1)
                link(dve.tensor_reduce(lmax[:, :], logits, AX_X, ALU.max))
                dve.tensor_tensor(lex[:, :, :], logits,
                                  lmax[:, :].unsqueeze(2).to_broadcast([P, TT, NR]),
                                  ALU.subtract).then_inc(r_sub, 1)
                dve.wait_ge(r_exp, b + 1)
                link(dve.tensor_reduce(lsum[:, :], lexp[:, :, :], AX_X, ALU.add))
                link(dve.reciprocal(linv[:, :], lsum[:, :]))
                if b == 0:
                    dve.wait_ge(pool_init, 1)
                link(dve.tensor_tensor(pr[:, :, 0:NR], lexp[:, :, :],
                                       linv[:, :].unsqueeze(2).to_broadcast([P, TT, NR]), ALU.mult))
                for t in range(TT):
                    last = dve.max(top[:, t, :], pr[:, t, 0:NR])
                link(last)
                link(dve.memset(top[:, :, TOPK:8], -1.0))
                for t in range(TT):
                    last = dve.match_replace(rep[:, t, :], top[:, t, :], pr[:, t, :], -2.0)
                link(last)
                if b:
                    dve.wait_ge(gT_pe, b)
                dve.scalar_tensor_tensor(gate[:, :, :], rep[:, :, 0:NR], -1.5, pr[:, :, 0:NR],
                                         ALU.is_lt, ALU.mult).then_inc(r_gate, 1)

            def do(job):
                kind, n = job
                if kind == "w" and n < 3:
                    dve.wait_ge(w_hi, n + 1)
                    dve.tensor_tensor(wl[:, slot(n), :], raw[:, n % RAW, :],
                                      wh[:, slot(n), :].bitcast(F32), ALU.subtract
                                      ).then_inc(w_lo_v, 1)
                elif kind == "ctx" and n == 0:
                    dve.wait_ge(c_hi, 1)
                    dve.tensor_tensor(xTl[1][:, :, :], craw[:, :, :], xTh[1][:, :, :].bitcast(F32),
                                      ALU.subtract).then_inc(c_lo, 1)
                elif kind == "stat":
                    statistics(n)
                elif kind == "norm":
                    normalise(n)
                elif kind == "xT":
                    rest_bank_pair(xTl[side(n)], xTh[side(n)], job, xT_hi, xT_lo)
                elif kind in "qk":
                    rotate(job)
                elif kind == "y":
                    b = n // GROUPS
                    dve.wait_ge(y_pe, n + 1)
                    if n:
                        dve.wait_ge(y_out, n)
                    else:
                        dve.wait_ge(tg_done, 1)
                    dve.scalar_tensor_tensor(x[:, b, :, :].rearrange("p t d -> p (t d)"),
                                             both_banks(job)[:, :, :].rearrange("p a n -> p (a n)"),
                                             tg[:, 0:1], x[:, b, :, :].rearrange("p t d -> p (t d)"),
                                             ALU.mult, ALU.add).then_inc(y_out, 1)
                elif kind == "r":
                    router(n)
                elif kind == "gT":
                    dve.wait_ge(gT_pe, n + 1)
                    if n:
                        dve.wait_ge(gT_dram, 16 * n)
                    dve.tensor_copy(gT, banks(job)[0][0:NR, :]).then_inc(gT_out, 1)
                elif kind == "z":
                    dve.wait_ge(down_pe, NE * (n + 1))
                    for i in range(2):
                        last = dve.scalar_tensor_tensor(
                            x[:, n, 2 * i:2 * i + 2, :].rearrange("p t d -> p (t d)"),
                            psS[i][:, :, :].rearrange("p t c -> p (t c)"), tg[:, 1:2],
                            x[:, n, 2 * i:2 * i + 2, :].rearrange("p t d -> p (t d)"),
                            ALU.mult, ALU.add)
                    last.then_inc(z_out, 1)

            def score_max(c):
                dve.wait_ge(s_pe, c + 1)
                if c == 0:
                    dve.wait_ge(in_const, consts)
                if c >= 2:
                    dve.wait_ge(s_exp, c - 1)
                for t in range(TT):
                    last = dve.tensor_tensor_reduce(sneg[:, c % 2, t, :], psS[c % 2][:, t, :],
                                                    mask[:, min(t, 1), :], -SCALE, -MASKED * 1e3,
                                                    ALU.add, ALU.min, nmax[:, c % 4, t:t + 1])
                last.then_inc(s_max, 1)

            def divide(c):
                dve.wait_ge(s_exp, c + 1)
                if c:
                    dve.wait_ge(s_norm, c)
                dve.reciprocal(rinv[:, c % 2, :], rsum[:, c % 4, :]).then_inc(s_inv, 1)
                dve.wait_ge(s_inv, c + 1)
                dve.tensor_tensor(prob[:, c % 3, :, :], prob[:, c % 3, :, :],
                                  rinv[:, c % 2, :].unsqueeze(2).to_broadcast([P, TT, P]),
                                  ALU.mult).then_inc(s_norm, 1)

            def rest_att(p):
                dve.wait_ge(oT_hi, p + 1)
                dve.tensor_tensor(oTl[:, p % 2, :], psO[:, :], oTh[:, p % 2, :].bitcast(F32),
                                  ALU.subtract).then_inc(oT_lo, 1)

            for job in prologue:
                do(job)
            dve.wait_ge(rw_hi, 1)
            dve.tensor_tensor(rwl[:, :, :], rw[:, :, :], rwh[:, :, :].bitcast(F32),
                              ALU.subtract).then_inc(rw_lo, 1)
            for c, jobs in steps:
                if c < CHUNKS:
                    score_max(c)
                if 1 <= c <= CHUNKS:
                    divide(c - 1)
                if c in attended:
                    rest_att(attended[c])
                for job in jobs:
                    do(job)

            def gated(n):
                b, e = experts[n]
                r = e - NS
                dve.wait_ge(f_gelu, n + 1)
                dve.wait_ge(gate_in[r], 16 * (b + 1))
                dve.wait_ge(f_hi, n - 1)
                dve.tensor_tensor(act_f[:, n % 2, :], act_g[:, n % 2, :], gate_bc[:, r, :],
                                  ALU.mult).then_inc(f_mul, 1)

            def rest_gated(n):
                b, e = experts[n]
                dve.wait_ge(f_hi, n + 1)
                src = act_g if e < NS else act_f
                dve.tensor_tensor(oTl[:, n % 2, :], src[:, n % 2, :], oTh[:, n % 2, :].bitcast(F32),
                                  ALU.subtract).then_inc(f_lo, 1)

            for n in range(N + 2):
                if n < N and experts[n][1] >= NS:
                    gated(n)
                if 1 <= n <= N:
                    rest_gated(n - 1)
                for job in after[n]:
                    do(job)

        @block.tensor
        def _(pe):
            def product(out, stationary, moving, start=True, stop=True, check=False):
                n = len(stationary)
                for i, (s, m) in enumerate(zip(stationary, moving)):
                    for j, (a, b) in enumerate(products(s, m)):
                        last = pe.matmul(out, a, b, start=start and i == 0 and j == 0,
                                         stop=stop and i == n - 1 and j == 2,
                                         skip_group_check=check)
                return last

            def weights(i):
                pe.wait_ge(w_hi, i + 1)
                wait_w_lo(pe, i)

            def cols(i, a, n):
                return wh[:, slot(i), a:a + n], wl[:, slot(i), a:a + n]

            def claim(job):
                if job in ring_at:
                    if ring_at[job] >= 2:
                        pe.wait_ge(*released(ring_jobs[ring_at[job] - 2]))
                elif job[0] == "xT":
                    pe.wait_ge(p_out, CHUNKS)
                    pe.wait_ge(oT_lo, CHUNKS // 2)
                    if job[1] > B + 1:
                        pe.wait_ge(gT_out, job[1] - B)
                elif job[0] == "r":
                    pe.wait_ge(xT_lo, B + job[1] + 1)
                elif job[0] == "gT":
                    pe.wait_ge(r_sub, job[1] + 1)

            def do(job):
                kind, n = job
                if kind not in in_ring:
                    return
                claim(job)
                two = banks(job)
                if kind == "xT":
                    if n == 0:
                        pe.wait_ge(in_ident, 16)
                    pe.wait_ge(ln_norm, n + 1)
                    for kc in range(KC):
                        for t in range(TT):
                            last = pe.transpose(two[kc][:, t * P:(t + 1) * P],
                                                xn[:, t, kc * P:(kc + 1) * P], ident[:, :])
                    last.then_inc(xT_pe, 1)
                elif kind in "qk":
                    b, g = divmod(n, GROUPS)
                    i = 4 * g + (0 if kind == "k" else 2)
                    weights(i)
                    if kind == "q":
                        pe.wait_ge(xT_lo, b + 1)
                    else:
                        pe.wait_ge(c_lo, b + 1)
                    X = 0 if kind == "q" else 1
                    for half in range(2):
                        last = product(two[half], [cols(i, kc * D + half * P, P) for kc in range(KC)],
                                       [(xTh[X][:, kc, :], xTl[X][:, kc, :]) for kc in range(KC)])
                    last.then_inc(qk_pe["qk".index(kind)], 1)
                elif kind == "v":
                    b, g = divmod(n, GROUPS)
                    i = 4 * g + 1
                    weights(i)
                    pe.wait_ge(c_lo, b + 1)
                    for t in range(TT):
                        last = product(two[t // 2][:, (t % 2) * GD:(t % 2 + 1) * GD],
                                       [(xTh[1][:, kc, t * P:(t + 1) * P],
                                         xTl[1][:, kc, t * P:(t + 1) * P]) for kc in range(KC)],
                                       [cols(i, kc * D, D) for kc in range(KC)])
                    last.then_inc(v_pe, 1)
                elif kind == "y":
                    i = 4 * (n % GROUPS) + 3
                    weights(i)
                    pe.wait_ge(oT_lo, 2 * (n + 1))
                    for t in range(TT):
                        last = product(two[t // 2][:, (t % 2) * D:(t % 2 + 1) * D],
                                       [(oTh[:, j, t * P:(t + 1) * P], oTl[:, j, t * P:(t + 1) * P])
                                        for j in range(2)],
                                       [cols(i, j * D, D) for j in range(2)])
                    last.then_inc(y_pe, 1)
                elif kind == "r":
                    pe.wait_ge(rw_lo, 1)
                    pe.wait_ge(xT_lo, B + n + 1)
                    X = side(B + n)
                    for t in range(TT):
                        last = product(two[0][:, t * NR:(t + 1) * NR],
                                       [(xTh[X][:, kc, t * P:(t + 1) * P],
                                         xTl[X][:, kc, t * P:(t + 1) * P]) for kc in range(KC)],
                                       [(rwh[:, kc, :], rwl[:, kc, :]) for kc in range(KC)])
                    last.then_inc(r_pe, 1)
                elif kind == "gT":
                    pe.wait_ge(r_gate, n + 1)
                    for t in range(TT):
                        last = pe.transpose(two[0][0:NR, t * P:(t + 1) * P], gate[:, t, :], ident[:, :])
                    last.then_inc(gT_pe, 1)

            def scores(c):
                u, h = divmod(c, G)
                rows = slice((h % 2) * DH, (h % 2) * DH + DH)
                if h == 0:
                    pe.wait_ge(qk_rot[0], u + 1)
                    pe.wait_ge(qk_rot[1], u + 1)
                if c >= 2:
                    pe.wait_ge(s_max, c - 1)
                for blk in range(L // W):
                    t, e = divmod(blk, 2)
                    last = pe.matmul(psS[c % 2][e * W:(e + 1) * W, t, :],
                                     qT[rows, u % 2, h // 2, blk * W:(blk + 1) * W],
                                     kT[rows, u % 2, h // 2, blk * W:(blk + 2) * W],
                                     start=True, stop=True)
                last.then_inc(s_pe, 1)

            def transpose_probs(c):
                pe.wait_ge(s_norm, c + 1)
                if c:
                    pe.wait_ge(p_out, c)
                for t in range(TT):
                    last = pe.transpose(psT[:, t, :], prob[:, c % 3, t, :], ident[:, :])
                last.then_inc(p_pe, 1)

            def values(p):
                u, pair = divmod(p, 2)
                pe.wait_ge(p_out, 2 * p + 2)
                if pair == 0:
                    pe.wait_ge(v_out, u + 1)
                    pe.wait_ge(v_in[u % 2], 32 * fillings(u))
                if p:
                    pe.wait_ge(oT_lo, p)
                else:
                    pe.wait_ge(pool_init, 1)
                for blk in range(L // W):
                    t, e = divmod(blk, 2)
                    v = v_al if e else v_sh
                    for h in range(2):
                        head = 2 * pair + h
                        last = pe.matmul(psO[h * DH:(h + 1) * DH, blk * W:(blk + 1) * W],
                                         v[:, u % 2, t, head * DH:(head + 1) * DH],
                                         pT[:, (2 * p + h) % 4, t, e * W:(e + 1) * W],
                                         start=True, stop=True)
                last.then_inc(oT_pe, 1)

            for job in prologue:
                do(job)
            for c, jobs in steps:
                if c < CHUNKS:
                    scores(c)
                if c in attended:
                    values(attended[c])
                for job in jobs:
                    do(job)
                if 2 <= c <= CHUNKS + 1:
                    transpose_probs(c - 2)

            def up(n):
                b, e = experts[n]
                i = expert_piece(e)
                if b == 0:
                    weights(i)
                if n < 4:
                    pe.wait_ge(*released(ring_jobs[-1]))
                    pe.wait_ge(*released(ring_jobs[-2]))
                else:
                    pe.wait_ge(f_gelu, n - 3)
                if e == 0:
                    pe.wait_ge(xT_lo, B + b + 1)
                X = side(B + b)
                product(ring[(n // 2) % 2][:, n % 2, :], [cols(i, kc * P, P) for kc in range(KC)],
                        [(xTh[X][:, kc, :], xTl[X][:, kc, :]) for kc in range(KC)]
                        ).then_inc(up_pe, 1)

            def down(n):
                b, e = experts[n]
                i = expert_piece(e)
                pe.wait_ge(f_lo, n + 1)
                if e == 0:
                    if b:
                        pe.wait_ge(z_out, b)
                    else:
                        pe.wait_ge(s_max, CHUNKS)
                for t in range(TT):
                    last = product(psS[t // 2][:, 2 * (t % 2):2 * (t % 2) + 2, :].rearrange("p a c -> p (a c)"),
                                   [(oTh[:, n % 2, t * P:(t + 1) * P], oTl[:, n % 2, t * P:(t + 1) * P])],
                                   [cols(i, D, D)], start=(e == 0 and t % 2 == 0), stop=(e == NE - 1),
                                   check=True)
                last.then_inc(down_pe, 1)

            for n in range(N + 2):
                if n < N:
                    up(n)
                if n >= 2:
                    down(n - 2)
                for job in after[n]:
                    do(job)


_OUT = ((B, L, D), "float32")


def tables():
    freqs = (1.0 / np.float32(ROPE_BASE) ** (np.arange(0, DH, 2, dtype=np.float32) / np.float32(DH)))
    ang = np.arange(L, dtype=np.float32)[:, None] * freqs.astype(np.float32)[None, :]
    row = np.arange(P)
    ang = ang[:, row % DH // QUAD * (QUAD // 2) + row % (QUAD // 2)].T
    cos = np.ascontiguousarray(np.cos(ang).astype(np.float32))
    sin = np.sin(ang).astype(np.float32) * np.where(row % QUAD < QUAD // 2, -1, 1).astype(np.float32)[:, None]
    r = np.arange(P)[:, None] % W
    c = np.arange(P)[None, :]
    seen = np.where(c < W, c >= r, c - W <= r)
    first = seen & ~((np.arange(P)[:, None] < W) & (c < W))
    mask = np.stack([np.where(m, 0.0, MASKED) for m in (first, seen)], 1).astype(np.float32)
    return cos, np.ascontiguousarray(sin), mask, np.eye(P, dtype=np.float32)


def kernel(x, ctx_1024, g_xattn, g_ffn, L0_xattn_wq, L0_xattn_wk, L0_xattn_wv, L0_xattn_wo,
           L0_ffn_shared_up, L0_ffn_shared_down, L0_ffn_routed_up, L0_ffn_routed_down,
           L0_ffn_router_w):
    import concourse.bacc as bacc
    from concourse.bass_utils import run_bass_kernel_spmd

    def a(v):
        return np.asarray(v)

    xt = a(x).reshape(B, TT, P, D).transpose(0, 2, 1, 3)
    ct = a(ctx_1024).reshape(B, L, KC, P).transpose(0, 3, 2, 1)
    wq, wk = (a(w).reshape(GROUPS, 2, 2, DH // QUAD, QUAD // 2, 2, KC, P)
              .transpose(0, 7, 6, 1, 2, 3, 5, 4).reshape(GROUPS, P, PIECE)
              for w in (L0_xattn_wq, L0_xattn_wk))
    wv = a(L0_xattn_wv).reshape(GROUPS, GD, KC, P).transpose(0, 3, 2, 1).reshape(GROUPS, P, PIECE)
    wo = a(L0_xattn_wo).reshape(D, GROUPS, 2, P).transpose(1, 3, 2, 0).reshape(GROUPS, P, PIECE)
    w = np.stack([wk, wv, wq, wo], 1).reshape(WPIECES, P, PIECE)
    up = np.concatenate([a(L0_ffn_shared_up), a(L0_ffn_routed_up)]).reshape(NE, P, KC, P)
    up = up.transpose(0, 3, 2, 1).reshape(NE, P, D)
    down = np.concatenate([a(L0_ffn_shared_down), a(L0_ffn_routed_down)]).transpose(0, 2, 1)
    e = np.concatenate([up, down], 2)
    rw = a(L0_ffn_router_w).reshape(NR, KC, P).transpose(2, 1, 0)
    cos, sin, mask, ident = tables()
    arrays = dict(x=xt, ctx=ct, gx=a(g_xattn), gf=a(g_ffn), w=w, e=e, rw=rw, cos=cos, sin=sin,
                  mask=mask, ident=ident)
    arrays = {f"in_{k}": np.ascontiguousarray(v) for k, v in arrays.items()}
    nc = bacc.Bacc("TRN2", target_bir_lowering=False, num_devices=1)
    args = [nc.dram_tensor(k, v.shape, F32, kind="ExternalInput").ap() for k, v in arrays.items()]
    args.append(nc.dram_tensor("out", (B, P, TT, D), F32, kind="ExternalOutput").ap())
    build(nc, *args)
    got = run_bass_kernel_spmd(nc, [arrays], core_ids=[0]).results[0]["out"]
    return np.asarray(got).reshape(B, P, TT, D).transpose(0, 2, 1, 3).reshape(B, L, D)
```

```python
from contextlib import ExitStack

import numpy as np

from concourse import mybir

F32 = mybir.dt.float32
F32R = mybir.dt.float32r
ALU = mybir.AluOpType
ACT = mybir.ActivationFunctionType
AX_X = mybir.AxisListType.X

P = 128
B, L, D = 4, 512, 256
H, DH, W = 16, 64, 64
QUAD = 32
ROPE_BASE = 10000.0
KC = D // P
TT = L // P
G = 4
GD = G * DH
GROUPS = H // G
UNITS = B * GROUPS
CHUNKS = UNITS * G
NS, NR, TOPK = 2, 16, 4
NE = NS + NR
SENT = 8 - TOPK
EPS = 1e-5
SCALE = float(DH) ** -0.5
MASKED = -1e30
PIECE = KC * D
WPIECES = 4 * GROUPS
RAW = 4
WARM_UP = 3
EARLY = 7


def products(stationary, moving):
    (sh, sl), (mh, ml) = stationary, moving
    return ((sh, mh), (sh, ml), (sl, mh))


def build(nc, x_d, ctx_d, gx_d, gf_d, w_d, e_d, rw_d, cos_d, sin_d, mask_d, ident_d, out_d):
    with ExitStack() as ctx:
        def sb(name, shape, dt=F32):
            return ctx.enter_context(nc.sbuf_tensor(name, shape, dt))

        def sem(name):
            return ctx.enter_context(nc.semaphore(name))

        x = sb("x", [P, B, TT, D])
        wh = sb("wh", [P, NE, PIECE], F32R)
        wl = sb("wl", [P, NE, PIECE], F32R)
        raw = sb("raw", [P, RAW, PIECE])
        xTh = [sb(f"xTh{i}", [P, KC, L], F32R) for i in range(2)]
        xTl = [sb(f"xTl{i}", [P, KC, L], F32R) for i in range(2)]
        craw = sb("craw", [P, KC, L])
        cos = sb("cos", [P, L])
        sin = sb("sin", [P, L])
        mask = sb("mask", [P, 2, P])
        ident = sb("ident", [P, P])
        xn = sb("xn", [P, TT, D])
        stats = sb("stats", [P, TT, 6])
        mv = sb("mv", [P, TT, 2])
        vare = sb("vare", [P, TT])
        rstd = sb("rstd", [P, TT])
        mhalf = sb("mhalf", [P, TT])
        gates_in = sb("gates_in", [P, 2])
        tg = sb("tg", [P, 2])
        rw = sb("rw", [P, KC, NR])
        rw_parts = sb("rw_parts", [P, KC, 2, NR], F32R)
        sizes = dict(swap=(2, 2, L), qT=(2, 2, L), kT=(2, 2, W + L), spare=(1, 2, 896),
                     v_al=(2, TT, GD), v_sh=(2, TT, GD))
        arena = sb("arena", [P, sum(int(np.prod(s)) for s in sizes.values())])
        cuts, at = {}, 0
        for name, (a, b, c) in sizes.items():
            cuts[name] = arena[:, at:at + a * b * c].rearrange("p (a b c) -> p a b c", a=a, b=b)
            at += a * b * c
        idle = cuts["spare"][:, 0, 0, 0:L]
        swap = cuts["swap"]
        qT, kT = cuts["qT"], cuts["kT"]
        v_al, v_sh = cuts["v_al"], cuts["v_sh"]
        gate_bc = arena[:, 0:NR * L].rearrange("p (e n) -> p e n", e=NR)
        sneg = sb("sneg", [P, 2, TT, P])
        prob = sb("prob", [P, 3, TT, P])
        pT = sb("pT", [P, 4, TT, P])
        nmax = sb("nmax", [P, 4, TT])
        rsum = sb("rsum", [P, 4, TT])
        rinv = sb("rinv", [P, 2, TT])
        oTh = sb("oTh", [P, 2, L], F32R)
        oTl = sb("oTl", [P, 2, L], F32R)
        act_g = sneg[:, :, :, :].rearrange("p a t c -> p a (t c)")
        act_f = prob[:, :, :, :].rearrange("p a t c -> p a (t c)")
        lmax = sb("lmax", [P, TT])
        lex = sb("lex", [P, TT, NR])
        lexp = sb("lexp", [P, TT, NR])
        lsum = sb("lsum", [P, TT])
        linv = sb("linv", [P, TT])
        pr = sb("pr", [P, TT, NR + SENT])
        top = sb("top", [P, TT, 8])
        rep = sb("rep", [P, TT, NR + SENT])
        gate = sb("gate", [P, TT, NR])
        gT = craw[0:NR, 0, :]
        gT_d = nc.dram_tensor("gate_scratch", (B, NR, L), F32).ap()

        ring = [ctx.enter_context(nc.psum_tensor(f"ring{i}", [P, 2, L], F32)) for i in range(2)]
        psS = [ctx.enter_context(nc.psum_tensor(f"psS{i}", [P, TT, P], F32)) for i in range(2)]
        psT = ctx.enter_context(nc.psum_tensor("psT", [P, TT, P], F32))
        psO = ctx.enter_context(nc.psum_tensor("psO", [P, L], F32))

        in_x = [sem(f"in_x{b}") for b in range(B)]
        in_ctx = sem("in_ctx")
        in_raw = [sem(f"in_raw{i}") for i in range(RAW)]
        in_ident, in_rope = sem("in_ident"), sem("in_rope")
        in_const = sem("in_const")
        idle_set = sem("idle_set")
        pool_init = sem("pool_init")
        w_hi = sem("w_hi")
        w_lo_v = sem("w_lo_v")
        w_lo_p = sem("w_lo_p")
        rw_hi, rw_lo = sem("rw_hi"), sem("rw_lo")
        c_hi, c_lo = sem("c_hi"), sem("c_lo")
        tg_done = sem("tg_done")
        ln_stat = sem("ln_stat")
        ln_rstd = sem("ln_rstd")
        ln_norm = sem("ln_norm")
        xT_pe, xT_hi, xT_lo = sem("xT_pe"), sem("xT_hi"), sem("xT_lo")
        qk_pe = [sem("q_pe"), sem("k_pe")]
        qk_swap = [sem("q_swap"), sem("k_swap")]
        qk_mul = [sem("q_mul"), sem("k_mul")]
        qk_rot = [sem("q_rot"), sem("k_rot")]
        v_pe, v_out = sem("v_pe"), sem("v_out")
        v_in = [sem(f"v_in{i}") for i in range(2)]
        s_pe, s_max, s_exp = sem("s_pe"), sem("s_max"), sem("s_exp")
        s_inv, s_norm = sem("s_inv"), sem("s_norm")
        p_pe, p_out = sem("p_pe"), sem("p_out")
        oT_pe, oT_hi, oT_lo = sem("oT_pe"), sem("oT_hi"), sem("oT_lo")
        y_pe, y_out = sem("y_pe"), sem("y_out")
        dve_link, pool_link = sem("dve_link"), sem("pool_link")
        r_pe, r_sub, r_exp, r_gate = sem("r_pe"), sem("r_sub"), sem("r_exp"), sem("r_gate")
        gT_pe, gT_out, gT_dram = sem("gT_pe"), sem("gT_out"), sem("gT_dram")
        gate_in = [sem(f"gate_in{i}") for i in range(NR)]
        up_pe, f_gelu, f_mul = sem("up_pe"), sem("f_gelu"), sem("f_mul")
        f_hi, f_lo, down_pe = sem("f_hi"), sem("f_lo"), sem("down_pe")
        z_out, out_done = sem("z_out"), sem("out_done")

        def slot(i):
            return i if i < NE else i - NE

        def expert_piece(e):
            return WPIECES + e

        prologue = [("ctx", 0), ("w", 0), ("stat", 0), ("w", 1), ("norm", 0), ("w", 2), ("k", 0),
                    ("v", 0), ("xT", 0), ("warm", 2), ("w", 3), ("w", 4), ("q", 0), ("w", 5), ("w", 6),
                    ("k", 1), ("warm", 3)]
        steps = []
        for c in range(CHUNKS + 4):
            u, k = divmod(c, 4)
            b, g = divmod(u, GROUPS)
            jobs = []
            if k == 0 and u + 1 < UNITS:
                jobs.append(("q", u + 1))
            if k == 1 and 1 <= u and u + 1 < UNITS:
                jobs.append(("k", u + 1))
            if (u, k) == (0, 1) or (k == 2 and 1 <= u and u + 1 < UNITS):
                jobs.append(("v", u + 1))
            if k == 2 and g == 2 and b + 1 < B:
                jobs.append(("xT", b + 1))
            if k == 3 and u >= 1:
                jobs.append(("y", u - 1))
            if k == 3 and g == 2 and b + 1 < B:
                jobs.append(("ctx", b + 1))
            if (u, k) == (0, 1):
                jobs.append(("w", EARLY))
            if (u, k) == (0, 3):
                jobs.append(("warm", 1))
            if u < 2 and k >= 2:
                jobs += [("w", 8 + 4 * u + 2 * (k - 2)), ("w", 9 + 4 * u + 2 * (k - 2))]
            if k == 3 and g == 1 and b + 1 < B:
                jobs.append(("stat", b + 1))
            if k == 0 and g == 2 and b + 1 < B:
                jobs.append(("norm", b + 1))
            jobs += {(UNITS - 3, 1): [("stat", B)], (UNITS - 3, 3): [("norm", B)],
                     (UNITS - 2, 3): [("xT", B)], (UNITS - 1, 0): [("r", 0)],
                     (UNITS - 1, 1): [("pick", 0)],
                     (UNITS - 1, 2): [("gT", 0)]}.get((u, k), [])
            if (u, k) == (UNITS - 4, 0):
                jobs += [("w", expert_piece(e)) for e in range(NS)]
            if UNITS - 2 <= u < UNITS:
                jobs.append(("w", expert_piece(NS + 4 * (u - (UNITS - 2)) + k)))
            if u == UNITS:
                jobs.append(("spread", k))
            if u == UNITS and 1 <= k <= NS:
                jobs.append(("expert", k - 1))
            steps.append((c, jobs))
        attended = {2 * p + 4: p for p in range(CHUNKS // 2)}
        experts = [(b, e) for b in range(B) for e in range(NE)]
        N = len(experts)
        after = {n: [] for n in range(N + 2)}
        for e in range(NS + 8, NE):
            after[e - 8].append(("w", expert_piece(e)))
        for b in range(B - 1):
            for e, kind in ((5, "stat"), (6, "norm"), (8, "xT"), (10, "r"), (12, "pick"), (14, "gT")):
                after[b * NE + e].append((kind, b + 1 + (B if kind in ("stat", "norm", "xT") else 0)))
            after[b * NE + 14] += [("spread", 4 * (b + 1) + quarter) for quarter in range(4)]
        for b in range(B):
            after[b * NE + NE + 1].append(("z", b))

        in_ring = ("xT", "q", "k", "v", "y", "r", "gT")
        jobs_a = [j for jobs in [prologue] + [jobs for _, jobs in steps] for j in jobs]
        ring_jobs = [j for j in jobs_a if j[0] in in_ring and j != ("xT", 0)]
        ring_at = {j: n - len(ring_jobs) % 2 for n, j in enumerate(ring_jobs)}

        def banks(job):
            if job in ring_at:
                r = ring[ring_at[job] % 2]
                return [r[:, 0, :], r[:, 1, :]]
            return [psT[:, :, :].rearrange("p t c -> p (t c)"),
                    psO[:, :]]

        def both_banks(job):
            return ring[ring_at[job] % 2]

        def rotated(u, pair=1):
            return pair + 1 if u == 0 else u + 2

        def rotations(u):
            if u == 0:
                return [(rotated(0, pair), slice(pair, pair + 1)) for pair in range(2)]
            return [(rotated(u), slice(0, 2))]

        def released(job):
            kind, n = job
            return {"xT": (xT_lo, n + 1), "q": (qk_mul[0], rotated(n)), "k": (qk_mul[1], rotated(n)),
                    "v": (v_out, n + 1), "y": (y_out, n + 1),
                    "r": (r_sub, n + 1), "gT": (gT_out, n + 1)}[kind]

        def fillings(u):
            return u // 2 + 1

        def side(j):
            return 0 if j < B else (j - B) % 2

        def wait_w_lo(eng, i):
            if i < EARLY:
                eng.wait_ge(w_lo_v, i + 1)
            else:
                eng.wait_ge(w_lo_p, i - EARLY + 1)

        def wait_slot_free(eng, i):
            if i >= NE:
                g, m = divmod(slot(i), 4)
                eng.wait_ge(y_pe if m == 3 else v_pe, (B - 1) * GROUPS + g + 1)

        def gated_parts(n):
            if n < NS:
                return xTh[1][:, n, :], xTl[1][:, n, :]
            return oTh[:, n % 2, :], oTl[:, n % 2, :]

        def sums(b, half):
            if b % 2:
                return ring[1][:, half, :]
            return psS[half][:, :, :].rearrange("p t c -> p (t c)")

        consts = 16 * 4
        block = ctx.enter_context(nc.Block())

        @block.sync
        def _(sp):
            def load_piece(i):
                if i >= RAW:
                    sp.wait_ge(w_hi, i - RAW + 1)
                    wait_w_lo(sp, i - RAW)
                src = w_d[i] if i < WPIECES else e_d[i - WPIECES]
                sp.dma_start(raw[:, i % RAW, :], src).then_inc(in_raw[i % RAW], 16)

            def load_ctx(b):
                if b:
                    sp.wait_ge(c_lo, b)
                sp.dma_start(craw[:, :, :], ctx_d[b]).then_inc(in_ctx, 16)

            def shift_values(u):
                sp.wait_ge(v_out, u + 1)
                sp.dma_start(v_sh[W:P, u % 2, :, :], v_al[0:W, u % 2, :, :]).then_inc(v_in[u % 2], 16)
                sp.dma_start(v_sh[0:W, u % 2, 1:TT, :],
                             v_al[W:P, u % 2, 0:TT - 1, :]).then_inc(v_in[u % 2], 16)

            def spread_gates(n):
                b, quarter = divmod(n, 4)
                if quarter == 0:
                    sp.wait_ge(gT_out, b + 1)
                    sp.dma_start(gT_d[b], gT).then_inc(gT_dram, 16)
                    sp.wait_ge(gT_dram, 16 * (b + 1))
                for r in range(quarter * NR // 4, (quarter + 1) * NR // 4):
                    if b:
                        sp.wait_ge(f_mul, (b - 1) * NR + r + 1)
                    elif r == 0:
                        sp.wait_ge(s_pe, CHUNKS)
                    sp.dma_start(gate_bc[:, r, :],
                                 gT_d[b, r].partition_broadcast(P)).then_inc(gate_in[r], 16)

            load_ctx(0)
            load_piece(0)
            sp.dma_start(x[:, 0, :, :], x_d[0]).then_inc(in_x[0], 16)
            sp.dma_start(ident[:, :], ident_d).then_inc(in_ident, 16)
            load_piece(1)
            load_piece(2)
            sp.dma_start(cos[:, :], cos_d).then_inc(in_rope, 16)
            sp.dma_start(sin[:, :], sin_d).then_inc(in_rope, 16)
            load_piece(3)
            for dst, src in ((mask[:, :, :], mask_d), (rw[:, :, :], rw_d),
                             (gates_in[:, 0:1], gx_d.partition_broadcast(P)),
                             (gates_in[:, 1:2], gf_d.partition_broadcast(P))):
                sp.dma_start(dst, src).then_inc(in_const, 16)
            def store(b):
                for half in range(2):
                    sp.wait_ge(z_out, 2 * b + half + 1)
                    sp.dma_start(out_d[b][:, 2 * half:2 * half + 2, :],
                                 x[:, b, 2 * half:2 * half + 2, :]).then_inc(out_done, 16)

            def do(job):
                kind, n = job
                if kind == "w" and n + RAW < WPIECES + NE:
                    load_piece(n + RAW)
                elif kind == "q" and n % GROUPS == 0 and n // GROUPS + 1 < B:
                    b = n // GROUPS + 1
                    sp.dma_start(x[:, b, :, :], x_d[b]).then_inc(in_x[b], 16)
                    load_ctx(b)
                elif kind == "v":
                    shift_values(n)
                elif kind == "spread":
                    spread_gates(n)
                elif kind == "z":
                    store(n)

            for job in jobs_a + [j for n in range(NS, N + 2) for j in after[n]]:
                do(job)
            sp.wait_ge(out_done, 16 * 2 * B)

        @block.gpsimd
        def _(pool):
            links = [0]

            def link(ins):
                links[0] += 1
                ins.then_inc(pool_link, 1)
                pool.wait_ge(pool_link, links[0])

            pool.memset(idle[:, :], 0.0).then_inc(idle_set, 1)
            pool.memset(kT[:, :, :, 0:W], 0.0)
            pool.memset(v_sh[0:W, :, 0, :], 0.0)
            pool.memset(pr[:, :, NR:], -1.0)
            pool.memset(mhalf[:, :], -0.5).then_inc(pool_init, 1)
            pool.wait_ge(pool_init, 1)

            def do(job):
                kind, n = job
                if kind == "w" and n >= EARLY:
                    pool.wait_ge(w_hi, n + 1)
                    pool.tensor_tensor(wl[:, slot(n), :], raw[:, n % RAW, :],
                                       wh[:, slot(n), :].bitcast(F32),
                                       ALU.subtract).then_inc(w_lo_p, 1)
                elif kind == "ctx" and n:
                    pool.wait_ge(c_hi, n + 1)
                    pool.tensor_tensor(xTl[1][:, :, :], craw[:, :, :], xTh[1][:, :, :].bitcast(F32),
                                       ALU.subtract).then_inc(c_lo, 1)
                elif kind in "qk":
                    i = "qk".index(kind)
                    dst = qT[:, n % 2, :, :] if kind == "q" else kT[:, n % 2, :, W:]
                    if n == 0:
                        pool.wait_ge(in_rope, 32)
                    for done, pairs in rotations(n):
                        part = swap[:, i, pairs, :]
                        pool.wait_ge(qk_swap[i], done)
                        link(pool.tensor_tensor(part, part,
                                                sin[:, :].unsqueeze(1).to_broadcast(part.shape),
                                                ALU.mult))
                        pool.wait_ge(qk_mul[i], done)
                        pool.tensor_tensor(dst[:, pairs, :], dst[:, pairs, :], part,
                                           ALU.add).then_inc(qk_rot[i], 1)
                elif kind == "stat":
                    pool.wait_ge(ln_stat, n + 1)
                    link(pool.tensor_scalar(vare[:, :], mv[:, :, 1], EPS, None, ALU.add))
                    pool.tensor_tensor(rstd[:, :], vare[:, :], mhalf[:, :],
                                       ALU.pow).then_inc(ln_rstd, 1)

            for job in jobs_a + [j for n in range(NS, N + 2) for j in after[n]]:
                do(job)

        @block.scalar
        def _(act):

            def round_bank_pair(dst, job, ready, done):
                act.wait_ge(ready, job[1] + 1)
                two = banks(job)
                if job in ring_at:
                    act.activation(dst[:, :, :], both_banks(job)[:, :, :], ACT.Copy).then_inc(done, 1)
                else:
                    act.activation(dst[:, 0, :], two[0], ACT.Copy)
                    act.activation(dst[:, 1, :], two[1], ACT.Copy).then_inc(done, 1)

            def gelu(n):
                act.wait_ge(up_pe, n + 1)
                if n >= 2:
                    act.wait_ge(f_lo, n - 1)
                act.activation(act_g[:, n % 2, :], ring[0][:, n % 2, :],
                               ACT.Gelu).then_inc(f_gelu, 1)

            def round_gated(n):
                b, e = experts[n]
                if e < NS:
                    act.wait_ge(f_gelu, n + 1)
                else:
                    act.wait_ge(f_mul, b * NR + e - NS + 1)
                if n < NS:
                    act.wait_ge(v_pe, UNITS)
                elif n < NS + 2:
                    act.wait_ge(y_pe, UNITS)
                else:
                    act.wait_ge(down_pe, 2 * (n - 1))
                src = act_g if e < NS else act_f
                act.activation(gated_parts(n)[0], src[:, n % 2, :], ACT.Copy).then_inc(f_hi, 1)

            def expert(n):
                if n < N:
                    gelu(n)
                if 1 <= n <= N:
                    round_gated(n - 1)

            def do(job):
                kind, n = job
                if kind == "w":
                    act.wait_ge(in_raw[n % RAW], 16 * (n // RAW + 1))
                    wait_slot_free(act, n)
                    act.activation(wh[:, slot(n), :], raw[:, n % RAW, :], ACT.Copy).then_inc(w_hi, 1)
                elif kind == "ctx":
                    act.wait_ge(in_ctx, 16 * (n + 1))
                    if n:
                        act.wait_ge(v_pe, GROUPS * n)
                    act.activation(xTh[1][:, :, :], craw[:, :, :], ACT.Copy).then_inc(c_hi, 1)
                elif kind == "xT":
                    round_bank_pair(xTh[side(n)], job, xT_pe, xT_hi)
                elif kind == "v":
                    act.wait_ge(v_pe, n + 1)
                    if n >= 2:
                        act.wait_ge(oT_pe, 2 * (n - 1))
                        act.wait_ge(v_in[n % 2], 32 * (fillings(n) - 1))
                    act.activation(v_al[:, n % 2, :, :].rearrange("p t d -> p (t d)"),
                                   both_banks(job)[:, :, :].rearrange("p a n -> p (a n)"),
                                   ACT.Copy).then_inc(v_out, 1)
                elif kind == "expert":
                    expert(n)
                elif kind == "r":
                    act.wait_ge(r_sub, n + 1)
                    act.activation(lexp[:, :, :], lex[:, :, :], ACT.Exp).then_inc(r_exp, 1)

            def softmax_numerator(c):
                act.wait_ge(s_max, c + 1)
                if c >= 3:
                    act.wait_ge(p_pe, c - 2)
                for t in range(TT):
                    last = act.activation(prob[:, c % 3, t, :], sneg[:, c % 2, t, :], ACT.Exp,
                                          bias=nmax[:, c % 4, t:t + 1], scale=-1.0,
                                          accum_out=rsum[:, c % 4, t:t + 1])
                last.then_inc(s_exp, 1)

            def copy_transposed(c):
                act.wait_ge(p_pe, c + 1)
                if c >= 4:
                    act.wait_ge(oT_pe, c // 2 - 1)
                act.activation(pT[:, c % 4, :, :], psT[:, :, :], ACT.Copy).then_inc(p_out, 1)

            def round_att(p):
                act.wait_ge(oT_pe, p + 1)
                if p >= 2:
                    act.wait_ge(y_pe, p // 2)
                act.activation(oTh[:, p % 2, :], psO[:, :], ACT.Copy).then_inc(oT_hi, 1)

            for job in prologue:
                do(job)
            act.wait_ge(in_const, consts)
            act.activation(tg[:, :], gates_in[:, :], ACT.Tanh).then_inc(tg_done, 1)
            act.activation(rw_parts[:, :, 0, :], rw[:, :, :], ACT.Copy).then_inc(rw_hi, 1)
            for c, jobs in steps:
                if 2 <= c <= CHUNKS + 1:
                    copy_transposed(c - 2)
                if c in attended:
                    round_att(attended[c])
                if c < CHUNKS:
                    softmax_numerator(c)
                for job in jobs:
                    do(job)

            for n in range(NS, N + 2):
                expert(n)
                for job in after[n]:
                    do(job)

        @block.vector
        def _(dve):
            links = [0]

            def link(ins):
                links[0] += 1
                ins.then_inc(dve_link, 1)
                dve.wait_ge(dve_link, links[0])

            def rest_bank_pair(dst, hi, job, hi_done, done):
                dve.wait_ge(hi_done, job[1] + 1)
                two = banks(job)
                if job in ring_at:
                    dve.tensor_tensor(dst[:, :, :], both_banks(job)[:, :, :], hi[:, :, :].bitcast(F32),
                                      ALU.subtract).then_inc(done, 1)
                else:
                    dve.tensor_tensor(dst[:, 0, :], two[0], hi[:, 0, :].bitcast(F32), ALU.subtract)
                    dve.tensor_tensor(dst[:, 1, :], two[1], hi[:, 1, :].bitcast(F32),
                                      ALU.subtract).then_inc(done, 1)

            def statistics(j):
                b = j % B
                if j < B:
                    dve.wait_ge(in_x[b], 16)
                else:
                    dve.wait_ge(y_out, GROUPS * (b + 1))
                for t in range(TT):
                    last = dve.bn_stats(stats[:, t, :], x[:, b, t, :])
                link(last)
                for t in range(TT):
                    last = dve.bn_aggr(mv[:, t, :], stats[:, t, :])
                last.then_inc(ln_stat, 1)

            def normalise(j):
                dve.wait_ge(ln_rstd, j + 1)
                if j:
                    dve.wait_ge(xT_pe, j)
                for t in range(TT):
                    last = dve.tensor_scalar(xn[:, t, :], x[:, j % B, t, :], mv[:, t, 0:1],
                                             rstd[:, t:t + 1], ALU.subtract, ALU.mult)
                last.then_inc(ln_norm, 1)

            def rotate(job):
                kind, u = job
                i = "qk".index(kind)
                dve.wait_ge(qk_pe[i], u + 1)
                if u == 0:
                    dve.wait_ge(in_rope, 32)
                else:
                    dve.wait_ge(qk_rot[i], rotated(u - 1))
                if u >= 2:
                    dve.wait_ge(s_pe, G * (u - 1))
                dst = qT[:, u % 2, :, :] if kind == "q" else kT[:, u % 2, :, W:]
                for _, pairs in rotations(u):
                    part = both_banks(job)[:, pairs, :]
                    dve.stream_shuffle(swap[:, i, pairs, :], part,
                                       [(lane + QUAD // 2) % QUAD for lane in range(QUAD)]
                                       ).then_inc(qk_swap[i], 1)
                    dve.tensor_tensor(dst[:, pairs, :], part,
                                      cos[:, :].unsqueeze(1).to_broadcast(part.shape),
                                      ALU.mult).then_inc(qk_mul[i], 1)

            def router(b):
                job = ("r", b)
                by_parts = banks(job)[0][:, 0:2 * TT * NR].rearrange("p (t a e) -> p t a e", t=TT, a=2)
                dve.wait_ge(r_pe, b + 1)
                link(dve.tensor_copy(lex[:, :, :], by_parts[:, :, 0, :]))
                link(dve.tensor_tensor(lex[:, :, :], lex[:, :, :], by_parts[:, :, 1, :], ALU.add))
                link(dve.tensor_reduce(lmax[:, :], lex[:, :, :], AX_X, ALU.max))
                dve.tensor_tensor(lex[:, :, :], lex[:, :, :],
                                  lmax[:, :].unsqueeze(2).to_broadcast([P, TT, NR]),
                                  ALU.subtract).then_inc(r_sub, 1)

            def pick(b):
                dve.wait_ge(r_exp, b + 1)
                link(dve.tensor_reduce(lsum[:, :], lexp[:, :, :], AX_X, ALU.add))
                link(dve.reciprocal(linv[:, :], lsum[:, :]))
                if b == 0:
                    dve.wait_ge(pool_init, 1)
                link(dve.tensor_tensor(pr[:, :, 0:NR], lexp[:, :, :],
                                       linv[:, :].unsqueeze(2).to_broadcast([P, TT, NR]), ALU.mult))
                for t in range(TT):
                    last = dve.max(top[:, t, :], pr[:, t, 0:NR])
                link(last)
                link(dve.memset(top[:, :, TOPK:8], -1.0))
                for t in range(TT):
                    last = dve.match_replace(rep[:, t, :], top[:, t, :], pr[:, t, :], -2.0)
                link(last)
                if b:
                    dve.wait_ge(gT_pe, b)
                dve.scalar_tensor_tensor(gate[:, :, :], rep[:, :, 0:NR], -1.5, pr[:, :, 0:NR],
                                         ALU.is_lt, ALU.mult).then_inc(r_gate, 1)

            def gated(n):
                b, e = experts[n]
                r = e - NS
                dve.wait_ge(f_gelu, n + 1)
                dve.wait_ge(gate_in[r], 16 * (b + 1))
                if b == 0 and r == 0:
                    dve.wait_ge(p_pe, CHUNKS)
                dve.wait_ge(f_hi, n - 1)
                dve.tensor_tensor(act_f[:, n % 2, :], act_g[:, n % 2, :], gate_bc[:, r, :],
                                  ALU.mult).then_inc(f_mul, 1)

            def rest_gated(n):
                b, e = experts[n]
                dve.wait_ge(f_hi, n + 1)
                hi, lo = gated_parts(n)
                src = act_g if e < NS else act_f
                dve.tensor_tensor(lo, src[:, n % 2, :], hi.bitcast(F32),
                                  ALU.subtract).then_inc(f_lo, 1)

            def expert(n):
                if n < N and experts[n][1] >= NS:
                    gated(n)
                if 1 <= n <= N:
                    rest_gated(n - 1)

            def do(job):
                kind, n = job
                if kind == "w" and n < EARLY:
                    dve.wait_ge(w_hi, n + 1)
                    dve.tensor_tensor(wl[:, slot(n), :], raw[:, n % RAW, :],
                                      wh[:, slot(n), :].bitcast(F32), ALU.subtract
                                      ).then_inc(w_lo_v, 1)
                elif kind == "ctx" and n == 0:
                    dve.wait_ge(c_hi, 1)
                    dve.tensor_tensor(xTl[1][:, :, :], craw[:, :, :], xTh[1][:, :, :].bitcast(F32),
                                      ALU.subtract).then_inc(c_lo, 1)
                elif kind == "stat":
                    statistics(n)
                elif kind == "norm":
                    normalise(n)
                elif kind == "xT":
                    rest_bank_pair(xTl[side(n)], xTh[side(n)], job, xT_hi, xT_lo)
                elif kind in "qk":
                    rotate(job)
                elif kind == "y":
                    b = n // GROUPS
                    dve.wait_ge(y_pe, n + 1)
                    if n:
                        dve.wait_ge(y_out, n)
                    else:
                        dve.wait_ge(tg_done, 1)
                    dve.scalar_tensor_tensor(x[:, b, :, :].rearrange("p t d -> p (t d)"),
                                             both_banks(job)[:, :, :].rearrange("p a n -> p (a n)"),
                                             tg[:, 0:1], x[:, b, :, :].rearrange("p t d -> p (t d)"),
                                             ALU.mult, ALU.add).then_inc(y_out, 1)
                elif kind == "r":
                    router(n)
                elif kind == "pick":
                    pick(n)
                elif kind == "gT":
                    dve.wait_ge(gT_pe, n + 1)
                    if n:
                        dve.wait_ge(gT_dram, 16 * n)
                    dve.tensor_copy(gT, banks(job)[0][0:NR, :]).then_inc(gT_out, 1)
                elif kind == "expert":
                    expert(n)
                elif kind == "z":
                    for half in range(2):
                        dve.wait_ge(down_pe, 2 * NE * (n + 1) - 1 + half)
                        tokens = x[:, n, 2 * half:2 * half + 2, :].rearrange("p t d -> p (t d)")
                        dve.scalar_tensor_tensor(tokens, sums(n, half), tg[:, 1:2], tokens,
                                                 ALU.mult, ALU.add).then_inc(z_out, 1)

            def score_max(c):
                dve.wait_ge(s_pe, c + 1)
                if c == 0:
                    dve.wait_ge(in_const, consts)
                if c >= 2:
                    dve.wait_ge(s_exp, c - 1)
                for t in range(TT):
                    last = dve.tensor_tensor_reduce(sneg[:, c % 2, t, :], psS[c % 2][:, t, :],
                                                    mask[:, min(t, 1), :], -SCALE, -MASKED * 1e3,
                                                    ALU.add, ALU.min, nmax[:, c % 4, t:t + 1])
                last.then_inc(s_max, 1)

            def divide(c):
                dve.wait_ge(s_exp, c + 1)
                if c:
                    dve.wait_ge(s_norm, c)
                dve.reciprocal(rinv[:, c % 2, :], rsum[:, c % 4, :]).then_inc(s_inv, 1)
                dve.wait_ge(s_inv, c + 1)
                dve.tensor_tensor(prob[:, c % 3, :, :], prob[:, c % 3, :, :],
                                  rinv[:, c % 2, :].unsqueeze(2).to_broadcast([P, TT, P]),
                                  ALU.mult).then_inc(s_norm, 1)

            def rest_att(p):
                dve.wait_ge(oT_hi, p + 1)
                dve.tensor_tensor(oTl[:, p % 2, :], psO[:, :], oTh[:, p % 2, :].bitcast(F32),
                                  ALU.subtract).then_inc(oT_lo, 1)

            for job in prologue:
                do(job)
            dve.wait_ge(rw_hi, 1)
            dve.tensor_tensor(rw_parts[:, :, 1, :], rw[:, :, :],
                              rw_parts[:, :, 0, :].bitcast(F32), ALU.subtract).then_inc(rw_lo, 1)
            for c, jobs in steps:
                if c < CHUNKS:
                    score_max(c)
                if 1 <= c <= CHUNKS:
                    divide(c - 1)
                if c in attended:
                    rest_att(attended[c])
                for job in jobs:
                    do(job)

            for n in range(NS, N + 2):
                expert(n)
                for job in after[n]:
                    do(job)

        @block.tensor
        def _(pe):
            def product(out, stationary, moving, start=True, stop=True, check=False):
                n = len(stationary)
                for i, (s, m) in enumerate(zip(stationary, moving)):
                    for j, (a, b) in enumerate(products(s, m)):
                        last = pe.matmul(out, a, b, start=start and i == 0 and j == 0,
                                         stop=stop and i == n - 1 and j == 2,
                                         skip_group_check=check)
                return last

            def weights(i):
                pe.wait_ge(w_hi, i + 1)
                wait_w_lo(pe, i)

            def cols(i, a, n):
                return wh[:, slot(i), a:a + n], wl[:, slot(i), a:a + n]

            def keep_warm(count, in_prologue=True):
                bank = psS[0][:, :, :].rearrange("p t c -> p (t c)") if in_prologue else psO[:, :]
                for _ in range(count):
                    pe.matmul(bank, idle[:, 0:P], idle[:, :],
                              start=True, stop=True)

            def claim(job):
                if job in ring_at:
                    at = ring_jobs.index(job)
                    if at >= 2:
                        pe.wait_ge(*released(ring_jobs[at - 2]))
                elif job[0] == "xT" and job[1]:
                    pe.wait_ge(p_out, CHUNKS)
                    pe.wait_ge(oT_lo, CHUNKS // 2)
                    if job[1] > B + 1:
                        pe.wait_ge(gT_out, job[1] - B)
                elif job[0] == "r":
                    pe.wait_ge(xT_lo, B + job[1] + 1)
                elif job[0] == "gT":
                    pe.wait_ge(r_sub, job[1] + 1)

            def up(n):
                b, e = experts[n]
                i = expert_piece(e)
                if b == 0:
                    weights(i)
                if n < 2:
                    pe.wait_ge(*released(ring_jobs[-2]))
                else:
                    pe.wait_ge(f_gelu, n - 1)
                if e == 0:
                    pe.wait_ge(xT_lo, B + b + 1)
                X = side(B + b)
                product(ring[0][:, n % 2, :], [cols(i, kc * P, P) for kc in range(KC)],
                        [(xTh[X][:, kc, :], xTl[X][:, kc, :]) for kc in range(KC)]
                        ).then_inc(up_pe, 1)

            def down(n):
                b, e = experts[n]
                i = expert_piece(e)
                pe.wait_ge(f_lo, n + 1)
                if e == 0:
                    if b >= 2:
                        pe.wait_ge(z_out, 2 * (b - 1))
                    elif b:
                        pe.wait_ge(*released(ring_jobs[-1]))
                    else:
                        pe.wait_ge(s_max, CHUNKS)
                hi, lo = gated_parts(n)
                for t in range(TT):
                    half, at = t // 2, (t % 2) * D
                    last = product(sums(b, half)[:, at:at + D],
                                   [(hi[:, t * P:(t + 1) * P], lo[:, t * P:(t + 1) * P])],
                                   [cols(i, D, D)], start=(e == 0 and t % 2 == 0), stop=(e == NE - 1),
                                   check=True)
                    if t % 2:
                        last.then_inc(down_pe, 1)

            def expert(n):
                if n < N:
                    up(n)
                if n >= 2:
                    down(n - 2)

            def do(job):
                kind, n = job
                if kind == "expert":
                    expert(n)
                if kind == "warm":
                    keep_warm(n, (kind, n) in prologue)
                if kind not in in_ring:
                    return
                claim(job)
                two = banks(job)
                if kind == "xT":
                    if n == 0:
                        pe.wait_ge(in_ident, 16)
                    pe.wait_ge(ln_norm, n + 1)
                    for kc in range(KC):
                        for t in range(TT):
                            last = pe.transpose(two[kc][:, t * P:(t + 1) * P],
                                                xn[:, t, kc * P:(kc + 1) * P], ident[:, :])
                    last.then_inc(xT_pe, 1)
                elif kind in "qk":
                    b, g = divmod(n, GROUPS)
                    i = 4 * g + (0 if kind == "k" else 2)
                    weights(i)
                    if kind == "q":
                        pe.wait_ge(xT_lo, b + 1)
                    else:
                        pe.wait_ge(c_lo, b + 1)
                    X = 0 if kind == "q" else 1
                    for half in range(2):
                        last = product(two[half], [cols(i, kc * D + half * P, P) for kc in range(KC)],
                                       [(xTh[X][:, kc, :], xTl[X][:, kc, :]) for kc in range(KC)])
                    last.then_inc(qk_pe["qk".index(kind)], 1)
                elif kind == "v":
                    b, g = divmod(n, GROUPS)
                    i = 4 * g + 1
                    weights(i)
                    pe.wait_ge(c_lo, b + 1)
                    for t in range(TT):
                        last = product(two[t // 2][:, (t % 2) * GD:(t % 2 + 1) * GD],
                                       [(xTh[1][:, kc, t * P:(t + 1) * P],
                                         xTl[1][:, kc, t * P:(t + 1) * P]) for kc in range(KC)],
                                       [cols(i, kc * D, D) for kc in range(KC)])
                    last.then_inc(v_pe, 1)
                elif kind == "y":
                    i = 4 * (n % GROUPS) + 3
                    weights(i)
                    pe.wait_ge(oT_lo, 2 * (n + 1))
                    for t in range(TT):
                        last = product(two[t // 2][:, (t % 2) * D:(t % 2 + 1) * D],
                                       [(oTh[:, j, t * P:(t + 1) * P], oTl[:, j, t * P:(t + 1) * P])
                                        for j in range(2)],
                                       [cols(i, j * D, D) for j in range(2)])
                    last.then_inc(y_pe, 1)
                elif kind == "r":
                    pe.wait_ge(rw_lo, 1)
                    pe.wait_ge(xT_lo, B + n + 1)
                    X = side(B + n)
                    for t in range(TT):
                        for kc in range(KC):
                            for part in (xTh[X], xTl[X]):
                                last = pe.matmul(two[0][:, t * 2 * NR:(t + 1) * 2 * NR],
                                                 part[:, kc, t * P:(t + 1) * P],
                                                 rw_parts[:, kc, :, :].rearrange("p a e -> p (a e)"),
                                                 start=kc == 0 and part is xTh[X],
                                                 stop=kc == KC - 1 and part is xTl[X])
                    last.then_inc(r_pe, 1)
                elif kind == "gT":
                    pe.wait_ge(r_gate, n + 1)
                    for t in range(TT):
                        last = pe.transpose(two[0][0:NR, t * P:(t + 1) * P], gate[:, t, :], ident[:, :])
                    last.then_inc(gT_pe, 1)

            def scores(c):
                u, h = divmod(c, G)
                rows = slice((h % 2) * DH, (h % 2) * DH + DH)
                if h == 0:
                    pe.wait_ge(qk_rot[0], rotated(u, 0))
                    pe.wait_ge(qk_rot[1], rotated(u, 0))
                if h == 2 and u == 0:
                    pe.wait_ge(qk_rot[0], rotated(u))
                    pe.wait_ge(qk_rot[1], rotated(u))
                if c >= 2:
                    pe.wait_ge(s_max, c - 1)
                for blk in range(L // W):
                    t, e = divmod(blk, 2)
                    last = pe.matmul(psS[c % 2][e * W:(e + 1) * W, t, :],
                                     qT[rows, u % 2, h // 2, blk * W:(blk + 1) * W],
                                     kT[rows, u % 2, h // 2, blk * W:(blk + 2) * W],
                                     start=True, stop=True)
                last.then_inc(s_pe, 1)

            def transpose_probs(c):
                pe.wait_ge(s_norm, c + 1)
                if c:
                    pe.wait_ge(p_out, c)
                for t in range(TT):
                    last = pe.transpose(psT[:, t, :], prob[:, c % 3, t, :], ident[:, :])
                last.then_inc(p_pe, 1)

            def values(p):
                u, pair = divmod(p, 2)
                pe.wait_ge(p_out, 2 * p + 2)
                if pair == 0:
                    pe.wait_ge(v_out, u + 1)
                    pe.wait_ge(v_in[u % 2], 32 * fillings(u))
                if p:
                    pe.wait_ge(oT_lo, p)
                else:
                    pe.wait_ge(pool_init, 1)
                for blk in range(L // W):
                    t, e = divmod(blk, 2)
                    v = v_al if e else v_sh
                    for h in range(2):
                        head = 2 * pair + h
                        last = pe.matmul(psO[h * DH:(h + 1) * DH, blk * W:(blk + 1) * W],
                                         v[:, u % 2, t, head * DH:(head + 1) * DH],
                                         pT[:, (2 * p + h) % 4, t, e * W:(e + 1) * W],
                                         start=True, stop=True)
                last.then_inc(oT_pe, 1)

            pe.wait_ge(idle_set, 1)
            keep_warm(WARM_UP)
            for job in prologue:
                do(job)
            for c, jobs in steps:
                if c < CHUNKS:
                    scores(c)
                if c in attended:
                    values(attended[c])
                if 2 <= c <= CHUNKS + 1:
                    transpose_probs(c - 2)
                for job in jobs:
                    do(job)

            for n in range(NS, N + 2):
                expert(n)
                for job in after[n]:
                    do(job)


_OUT = ((B, L, D), "float32")


def tables():
    freqs = (1.0 / np.float32(ROPE_BASE) ** (np.arange(0, DH, 2, dtype=np.float32) / np.float32(DH)))
    ang = np.arange(L, dtype=np.float32)[:, None] * freqs.astype(np.float32)[None, :]
    row = np.arange(P)
    ang = ang[:, row % DH // QUAD * (QUAD // 2) + row % (QUAD // 2)].T
    cos = np.ascontiguousarray(np.cos(ang).astype(np.float32))
    sin = np.sin(ang).astype(np.float32) * np.where(row % QUAD < QUAD // 2, -1, 1).astype(np.float32)[:, None]
    r = np.arange(P)[:, None] % W
    c = np.arange(P)[None, :]
    seen = np.where(c < W, c >= r, c - W <= r)
    first = seen & ~((np.arange(P)[:, None] < W) & (c < W))
    mask = np.stack([np.where(m, 0.0, MASKED) for m in (first, seen)], 1).astype(np.float32)
    return cos, np.ascontiguousarray(sin), mask, np.eye(P, dtype=np.float32)


def kernel(x, ctx_1024, g_xattn, g_ffn, L0_xattn_wq, L0_xattn_wk, L0_xattn_wv, L0_xattn_wo,
           L0_ffn_shared_up, L0_ffn_shared_down, L0_ffn_routed_up, L0_ffn_routed_down,
           L0_ffn_router_w):
    import concourse.bacc as bacc
    from concourse.bass_utils import run_bass_kernel_spmd

    def a(v):
        return np.asarray(v)

    xt = a(x).reshape(B, TT, P, D).transpose(0, 2, 1, 3)
    ct = a(ctx_1024).reshape(B, L, KC, P).transpose(0, 3, 2, 1)
    wq, wk = (a(w).reshape(GROUPS, 2, 2, DH // QUAD, QUAD // 2, 2, KC, P)
              .transpose(0, 7, 6, 1, 2, 3, 5, 4).reshape(GROUPS, P, PIECE)
              for w in (L0_xattn_wq, L0_xattn_wk))
    wv = a(L0_xattn_wv).reshape(GROUPS, GD, KC, P).transpose(0, 3, 2, 1).reshape(GROUPS, P, PIECE)
    wo = a(L0_xattn_wo).reshape(D, GROUPS, 2, P).transpose(1, 3, 2, 0).reshape(GROUPS, P, PIECE)
    w = np.stack([wk, wv, wq, wo], 1).reshape(WPIECES, P, PIECE)
    up = np.concatenate([a(L0_ffn_shared_up), a(L0_ffn_routed_up)]).reshape(NE, P, KC, P)
    up = up.transpose(0, 3, 2, 1).reshape(NE, P, D)
    down = np.concatenate([a(L0_ffn_shared_down), a(L0_ffn_routed_down)]).transpose(0, 2, 1)
    e = np.concatenate([up, down], 2)
    rw = a(L0_ffn_router_w).reshape(NR, KC, P).transpose(2, 1, 0)
    cos, sin, mask, ident = tables()
    arrays = dict(x=xt, ctx=ct, gx=a(g_xattn), gf=a(g_ffn), w=w, e=e, rw=rw, cos=cos, sin=sin,
                  mask=mask, ident=ident)
    arrays = {f"in_{k}": np.ascontiguousarray(v) for k, v in arrays.items()}
    nc = bacc.Bacc("TRN2", target_bir_lowering=False, num_devices=1)
    args = [nc.dram_tensor(k, v.shape, F32, kind="ExternalInput").ap() for k, v in arrays.items()]
    args.append(nc.dram_tensor("out", (B, P, TT, D), F32, kind="ExternalOutput").ap())
    build(nc, *args)
    got = run_bass_kernel_spmd(nc, [arrays], core_ids=[0]).results[0]["out"]
    return np.asarray(got).reshape(B, P, TT, D).transpose(0, 2, 1, 3).reshape(B, L, D)
```
